# Optimizing a Trainium2 kernel written in Bass

```python
import numpy as np
import jax
import jax.numpy as jnp

def _softmax(x, axis=-1):
    return jax.nn.softmax(x, axis=axis)

def _gelu(x):
    return jax.nn.gelu(x, approximate=True)

def _silu(x):
    return jax.nn.silu(x)

def _sigmoid(x):
    return jax.nn.sigmoid(x)

def _layernorm(x, axis=-1, eps=1e-05):
    m = jnp.mean(x, axis=axis, keepdims=True)
    v = jnp.var(x, axis=axis, keepdims=True)
    return (x - m) / jnp.sqrt(v + eps)

def _scatter_add(tgt, idx, src, axis=0):
    return tgt.at[idx].add(src)

def _segment_sum(src, seg, n):
    return jax.ops.segment_sum(src, seg, n)
kernel_name = 'mk_conv_attn_hybrid_d2_conv_nchw768_r2_1fb899'

def setup_inputs(seed: int=0):
    np.random.seed(seed)
    _w = jnp.asarray

    def _rec_inputs():
        import jax
        import jax.numpy as jnp
        _gk = jax.random.key(seed)
        x = -0.0002221 + 1 * jax.random.normal(jax.random.fold_in(_gk, 1), (8, 384, 32, 32), jnp.float32)
        return x
    x = _rec_inputs()

    def _L0_conv_setup():
        import jax, jax.numpy as jnp
        import numpy as np
        K = 7
        PAD = K // 2
        EPS = 1e-12

        def _offsets():
            offs = []
            offs += [(i, i) for i in range(K)]
            offs += [(i, K // 2) for i in range(K)]
            offs += [(i, K - 1 - i) for i in range(K)]
            offs += [(K // 2, i) for i in range(K)]
            return offs
        key = jax.random.key(seed)
        k1, k2, k3 = jax.random.split(key, 3)
        B, C, H, W = (8, 384, 32, 32)
        OUT_C = 384
        feature = jax.random.normal(k1, (B, C, H, W), dtype=jnp.float32)
        conv_w = jax.random.normal(k2, (OUT_C, C + 4 * K), dtype=jnp.float32) * 0.02
        conv_b = jax.random.normal(k3, (OUT_C,), dtype=jnp.float32) * 0.02
        return {'feature': feature, 'conv_w': conv_w, 'conv_b': conv_b}
    _L0_conv_all = _L0_conv_setup()
    _L0_conv_in = {k: v for k, v in _L0_conv_all.items() if k in ('conv_w', 'conv_b')}
    del _L0_conv_all

    def _L1_attn_setup():
        import jax, jax.numpy as jnp
        import numpy as np
        B, N, C = (2, 1024, 384)
        H = 12
        HD = C // H
        SCALE = HD ** (-0.5)
        key = jax.random.key(seed)
        ks = jax.random.split(key, 5)
        s = 1.0 / np.sqrt(C)
        return {'x': jax.random.normal(ks[0], (B, N, C), dtype=jnp.float32), 'Wq': jax.random.normal(ks[1], (C, C), dtype=jnp.float32) * s, 'Wk': jax.random.normal(ks[2], (C, C), dtype=jnp.float32) * s, 'Wv': jax.random.normal(ks[3], (C, C), dtype=jnp.float32) * s, 'Wo': jax.random.normal(ks[4], (C, C), dtype=jnp.float32) * s, 'bo': jnp.zeros((C,), dtype=jnp.float32)}
    _L1_attn_all = _L1_attn_setup()
    _L1_attn_in = {k: v for k, v in _L1_attn_all.items() if k in ('Wq', 'Wk', 'Wv', 'Wo', 'bo')}
    del _L1_attn_all

    def _L1_ffn_setup():
        import jax, jax.numpy as jnp
        import numpy as np
        B, S, D_IN, D_HID, D_OUT = (32, 256, 384, 1536, 384)
        key = jax.random.key(seed)
        k1, k2, k3, k4 = jax.random.split(key, 4)
        init_k = float(np.sqrt(1.0 / D_IN))
        init_k2 = float(np.sqrt(1.0 / D_HID))
        x = jax.random.normal(k1, (B, S, D_IN), dtype=jnp.float32)
        in_weight = jax.random.uniform(k2, (D_HID, D_IN), dtype=jnp.float32, minval=-init_k, maxval=init_k)
        in_bias = jax.random.uniform(k3, (D_HID,), dtype=jnp.float32, minval=-init_k, maxval=init_k)
        out_weight = jax.random.uniform(k4, (D_HID, D_OUT), dtype=jnp.float32, minval=-init_k2, maxval=init_k2)
        return {'x': x, 'in_weight': in_weight, 'in_bias': in_bias, 'out_weight': out_weight}
    _L1_ffn_all = _L1_ffn_setup()
    _L1_ffn_in = {k: v for k, v in _L1_ffn_all.items() if k in ('in_weight', 'in_bias', 'out_weight')}
    del _L1_ffn_all
    return {'x': x, 'L0_conv_conv_w': _L0_conv_in['conv_w'], 'L0_conv_conv_b': _L0_conv_in['conv_b'], 'L1_attn_Wq': _L1_attn_in['Wq'], 'L1_attn_Wk': _L1_attn_in['Wk'], 'L1_attn_Wv': _L1_attn_in['Wv'], 'L1_attn_Wo': _L1_attn_in['Wo'], 'L1_attn_bo': _L1_attn_in['bo'], 'L1_ffn_in_weight': _L1_ffn_in['in_weight'], 'L1_ffn_in_bias': _L1_ffn_in['in_bias'], 'L1_ffn_out_weight': _L1_ffn_in['out_weight']}

def reference(x, L0_conv_conv_w, L0_conv_conv_b, L1_attn_Wq, L1_attn_Wk, L1_attn_Wv, L1_attn_Wo, L1_attn_bo, L1_ffn_in_weight, L1_ffn_in_bias, L1_ffn_out_weight):
    import jax
    import jax.numpy as jnp

    def _L0_conv_ref(feature, conv_w, conv_b):
        import jax, jax.numpy as jnp
        import numpy as np
        K = 7
        PAD = K // 2
        EPS = 1e-12

        def _offsets():
            offs = []
            offs += [(i, i) for i in range(K)]
            offs += [(i, K // 2) for i in range(K)]
            offs += [(i, K - 1 - i) for i in range(K)]
            offs += [(K // 2, i) for i in range(K)]
            return offs
        b, c, h, w = feature.shape
        norm = jnp.sqrt(jnp.sum(feature * feature, axis=1, keepdims=True))
        feat_n = feature / jnp.maximum(norm, EPS)
        feat_pad = jnp.pad(feat_n, ((0, 0), (0, 0), (PAD, PAD), (PAD, PAD)))
        corr = jnp.stack([jnp.sum(feat_pad[:, :, r:h + r, cc:w + cc] * feat_n, axis=1) for r, cc in _offsets()], axis=1)
        x = jnp.concatenate([feature, corr], axis=1)
        out = jnp.einsum('bchw,oc->bohw', x, conv_w) + conv_b[None, :, None, None]
        return out

    def _L1_attn_ref(x, Wq, Wk, Wv, Wo, bo):
        import jax, jax.numpy as jnp
        import numpy as np
        B, N, C = (2, 1024, 384)
        H = 12
        HD = C // H
        SCALE = HD ** (-0.5)
        b, n, c = x.shape
        q = (x @ Wq.T).reshape(b, n, H, HD).transpose(0, 2, 1, 3)
        k = (x @ Wk.T).reshape(b, n, H, HD).transpose(0, 2, 1, 3)
        v = (x @ Wv.T).reshape(b, n, H, HD).transpose(0, 2, 1, 3)
        scores = jnp.einsum('bhqd,bhkd->bhqk', q, k) * SCALE
        probs = jax.nn.softmax(scores, axis=-1)
        out = jnp.einsum('bhqk,bhkd->bhqd', probs, v)
        out = out.transpose(0, 2, 1, 3).reshape(b, n, c)
        return out @ Wo.T + bo

    def _L1_ffn_ref(x, in_weight, in_bias, out_weight):
        import jax, jax.numpy as jnp
        import numpy as np
        B, S, D_IN, D_HID, D_OUT = (32, 256, 384, 1536, 384)
        lead = x.shape[:-1]
        xt = x.reshape(-1, in_weight.shape[1])
        h = jax.nn.gelu(jnp.einsum('td,hd->th', xt, in_weight) + in_bias, approximate=False)
        out = jnp.einsum('th,ho->to', h, out_weight)
        return out.reshape(*lead, out_weight.shape[1])

    def _gn(v, G=32, eps=1e-05):
        B_, C_, H_, W_ = v.shape
        g = v.reshape(B_, G, C_ // G, H_, W_)
        m = jnp.mean(g, axis=(2, 3, 4), keepdims=True)
        s = jnp.var(g, axis=(2, 3, 4), keepdims=True)
        return ((g - m) / jnp.sqrt(s + eps)).reshape(v.shape)

    def _ln_c(v, eps=1e-06):
        m = jnp.mean(v, axis=1, keepdims=True)
        s = jnp.var(v, axis=1, keepdims=True)
        return (v - m) / jnp.sqrt(s + eps)

    def _ln_t(v, eps=1e-05):
        m = jnp.mean(v, axis=-1, keepdims=True)
        s = jnp.var(v, axis=-1, keepdims=True)
        return (v - m) / jnp.sqrt(s + eps)

    def _to_tokens(v):
        B_, C_, H_, W_ = v.shape
        return v.reshape(B_, C_, H_ * W_).transpose(0, 2, 1)

    def _from_tokens(t, like):
        B_, C_, H_, W_ = like.shape
        return t.transpose(0, 2, 1).reshape(B_, C_, H_, W_)
    x = x + _L0_conv_ref(_gn(x), L0_conv_conv_w, L0_conv_conv_b)
    t = _to_tokens(x)
    t = t + _L1_attn_ref(_ln_t(t), L1_attn_Wq, L1_attn_Wk, L1_attn_Wv, L1_attn_Wo, L1_attn_bo)
    t = t + _L1_ffn_ref(_ln_t(t), L1_ffn_in_weight, L1_ffn_in_bias, L1_ffn_out_weight)
    x = _from_tokens(t, x)
    return x

_drawn_inputs = setup_inputs


def setup_inputs(seed=0):
    import zlib

    import numpy as np

    out = dict(_drawn_inputs(seed))
    spreads = {'L1_attn_bo': (0.0, 0.1)}
    factors = {'L1_ffn_in_bias': 5.834}
    for name, (base, spread) in spreads.items():
        noise = np.random.default_rng([zlib.crc32(name.encode()), seed]).standard_normal(out[name].shape)
        drawn = base * np.exp(spread * noise) if base else spread * noise
        out[name] = jnp.asarray(drawn.astype(out[name].dtype))
    for name, factor in factors.items():
        out[name] = (out[name] * factor).astype(out[name].dtype)
    return out
```

```python
from contextlib import ExitStack

import concourse.bass as bass
from concourse import mybir

F32 = mybir.dt.float32
F16 = mybir.dt.float16
ALU = mybir.AluOpType
ACT = mybir.ActivationFunctionType
AX_X = mybir.AxisListType.X

C = 384
NPIX = 1024
P = 128
KC = C // P
ROW = 32
BANK = 512
HALVES = NPIX // BANK
WSCALE = 256.0
PARTS = [(0, 0), (0, 1), (1, 0)]


def wait(eng, sem, value):
    if isinstance(value, int) and value <= 0:
        return
    eng.wait_ge(sem, value)


def wait_both(eng, first, second):
    ready = [(s, v if isinstance(v, int) else eng.to_reg(v)) for s, v in (first, second)]
    for s, v in ready:
        wait(eng, s, v)


class Names:

    def __init__(self, nc, ctx, prefix):
        self.nc, self.ctx, self.prefix = nc, ctx, prefix

    def sb(self, name, shape, dt=F32):
        return self.ctx.enter_context(self.nc.sbuf_tensor(f"{self.prefix}_{name}", shape, dt))

    def ps(self, name, shape, dt=F32):
        return self.ctx.enter_context(self.nc.psum_tensor(f"{self.prefix}_{name}", shape, dt))

    def sem(self, name):
        return self.ctx.enter_context(self.nc.semaphore(f"{self.prefix}_{name}"))


def image_tile(dram, image, lo=0, n=NPIX):
    return dram[bass.ds(image, 1), :, lo:lo + n].rearrange("a (k p) n -> p (a k) n", p=P)


K7 = 7
PAD = K7 // 2
REFERENCE_SHIFTS = ([(i - PAD, i - PAD) for i in range(K7)] + [(i - PAD, 0) for i in range(K7)]
                    + [(i - PAD, PAD - i) for i in range(K7)] + [(0, i - PAD) for i in range(K7)])
KINDS = 3


def forward_column(kind, dr):
    return kind + 1 if dr == 0 else (kind - 1) * dr


FORWARD = [(dr, forward_column(kind, dr)) for dr in range(PAD + 1) for kind in range(KINDS)]
NF = len(FORWARD)
SELF = REFERENCE_SHIFTS.count((0, 0))
CORR_ROWS = FORWARD + [(0, 0)] * SELF + [(-r, -c) for r, c in FORWARD]
NC = len(CORR_ROWS)
BACK = NF + SELF
CB = 32


def conv_stage(nc, x_in, w_main, w_corr, group_mean, masks, selectors, corr_start, out, n_images):
    EPS = 1e-5
    NORM_EPS = 1e-12
    WINDOW = (PAD + 1) * ROW
    PADDED = NPIX + PAD * ROW
    ctx = ExitStack()
    with ctx:
        N = Names(nc, ctx, "a")
        stage_w = N.sb("stage_w", [P, KC * C])
        stage_c = N.sb("stage_c", [NC + 1, C])
        wm = [N.sb(f"wm{s}", [P, KC, C], F16) for s in range(2)]
        wc = N.sb("wc", [3 * CB, C], F16)
        gmean = N.sb("gmean", [P, KC * KC, P])
        mask = N.sb("mask", [P, KINDS + 1, ROW])
        sel = N.sb("sel", [P, KINDS + 1, BACK])
        ones = N.sb("ones", [P, P])
        eps = N.sb("eps", [P, 1])
        x = [N.sb(f"x{p}", [P, KC, NPIX]) for p in range(2)]
        bn = N.sb("bn", [P, KC, HALVES, 6])
        mv = N.sb("mv", [P, KC, 2])
        gm = N.sb("gm", [P, KC])
        dm = N.sb("dm", [P, KC])
        ev = N.sb("ev", [P, KC])
        rs = N.sb("rs", [P, KC])
        f = N.sb("f", [P, KC, NPIX])
        sq = N.sb("sq", [P, KC, NPIX])
        fs = [[N.sb(f"fs{p}{s}", [P, KC, NPIX], F16) for s in range(2)] for p in range(2)]
        nrm = N.sb("nrm", [P, NPIX])
        fn = [[N.sb(f"fn{p}{s}", [P, KC, PADDED], F16) for s in range(2)] for p in range(2)]
        picked = N.sb("picked", [P, KINDS + 1, NPIX])
        cs = [N.sb(f"cs{p}", [3 * CB, NPIX], F16) for p in range(2)]
        ob = [N.sb(f"ob{p}", [P, KC, NPIX]) for p in range(2)]
        stat = N.ps("stat", [P, NPIX])
        gram = N.ps("gram", [P, NPIX])
        corr = N.ps("corr", [P, NPIX])
        conv = [N.ps(f"conv{k}", [P, BANK]) for k in range(2)]

        w_loaded = N.sem("w_loaded")
        c_loaded = N.sem("c_loaded")
        set_up = N.sem("set_up")
        x_loaded = [N.sem(f"x_loaded{p}") for p in range(2)]
        stored = [N.sem(f"stored{p}") for p in range(2)]
        mv_ready = N.sem("mv_ready")
        gmean_ready = N.sem("gmean_ready")
        spread = N.sem("spread")
        gvar_ready = N.sem("gvar_ready")
        gstd_ready = N.sem("gstd_ready")
        ginv_ready = N.sem("ginv_ready")
        f_ready = N.sem("f_ready")
        fhi_ready = N.sem("fhi_ready")
        flo_ready = N.sem("flo_ready")
        squared = N.sem("squared")
        ssq_ready = N.sem("ssq_ready")
        norm_ready = N.sem("norm_ready")
        clamped = N.sem("clamped")
        fn_ready = N.sem("fn_ready")
        fnhi_ready = N.sem("fnhi_ready")
        fnlo_ready = N.sem("fnlo_ready")
        gram_ready = N.sem("gram_ready")
        masked = N.sem("masked")
        corr_ready = N.sem("corr_ready")
        chi_ready = N.sem("chi_ready")
        clo_ready = N.sem("clo_ready")
        shifted = [N.sem(f"shifted{p}") for p in range(2)]
        conv_ready = N.sem("conv_ready")
        evicted = N.sem("evicted")
        block = ctx.enter_context(nc.Block())
        EV = KC * HALVES
        SETUP = 9

        def images(eng, stage1, stage2):
            step(None, 0, stage1, stage2)
            for i in range(3):
                step(i, i + 1, stage1, stage2)
            with eng.Fori(1, n_images // 2 - 1) as pair:
                step(2 * pair + 1, 2 * pair + 2, stage1, stage2, 1)
                step(2 * pair + 2, 2 * pair + 3, stage1, stage2, 0)
            step(n_images - 1, None, stage1, stage2)

        def step(now, ahead, stage1, stage2, parity=None):
            p = parity if parity is not None else (now % 2 if now is not None else 1 - ahead % 2)
            one = stage1(ahead, 1 - p) if ahead is not None else iter(())
            two = stage2(now, p) if now is not None else iter(())
            live = [one, two]
            while live:
                for part in list(live):
                    if next(part, "end") == "end":
                        live.remove(part)

        def times16(i, p, n=1):
            return 16 * n * ((i - p) // 2) if isinstance(i, int) else 8 * n * (i - p)

        @block.sync
        def _(sp):
            def load(i, p):
                sp.dma_start(x[p][:, :, :], image_tile(x_in, i)).then_inc(x_loaded[p], 16)

            load(0, 0)
            for dst, src in ((gmean[:, :, :], group_mean), (mask[:, :, :], masks),
                             (sel[:, :, :], selectors), (cs[0][:, :], corr_start),
                             (cs[1][:, :], corr_start)):
                sp.dma_start(dst, src).then_inc(c_loaded, 16)
            load(1, 1)
            sp.dma_start(stage_w[:, :].rearrange("p (k n) -> p k n", k=KC),
                         w_main.rearrange("(k p) n -> p k n", p=P)).then_inc(w_loaded, 16)
            sp.dma_start(stage_c[:, :], w_corr).then_inc(w_loaded, 16)

            def turn(i, p, more):
                wait_both(sp, (chi_ready, 2 * i + 2), (clo_ready, i + 1))
                for n, (dr, dc) in enumerate(FORWARD):
                    s = dr * ROW + dc
                    sp.dma_start(cs[p][BACK + n:BACK + n + 2 * CB + 1:CB, s:NPIX],
                                 cs[p][n:n + 2 * CB + 1:CB, 0:NPIX - s]).then_inc(shifted[p], 16)
                sp.wait_ge(evicted, EV * (i + 1))
                if more:
                    load(i + 2, p)
                sp.dma_start(image_tile(out, i), ob[p][:, :, :]).then_inc(stored[p], 16)

            turn(0, 0, True)
            turn(1, 1, True)
            with sp.Fori(1, n_images // 2 - 1) as pair:
                turn(2 * pair, 0, True)
                turn(2 * pair + 1, 1, True)
            turn(n_images - 2, 0, False)
            turn(n_images - 1, 1, False)
            for p in range(2):
                sp.wait_ge(stored[p], 16 * (n_images // 2))

        @block.tensor
        def _(pe):
            def average(dst, column, source, done):
                for j in range(KC):
                    for k in range(KC):
                        last = nc.tensor.matmul(dst[:, column + j:column + j + 1], gmean[:, k * KC + j, :],
                                                source(k), start=k == 0, stop=k == KC - 1)
                last.then_inc(done, 1)

            def stage1(i, p):
                pe.wait_ge(mv_ready, i + 1)
                wait(pe, norm_ready, i)
                average(stat, 0, lambda k: mv[:, k, 0:1], gmean_ready)
                yield
                pe.wait_ge(spread, 3 * i + 3)
                average(stat, BANK, lambda k: ev[:, k:k + 1], gvar_ready)
                yield
                pe.wait_ge(squared, i + 1)
                pe.wait_ge(gstd_ready, i + 1)
                for h in range(HALVES):
                    for k in range(KC):
                        last = nc.tensor.matmul(stat[:, h * BANK:(h + 1) * BANK], ones[:, :],
                                                sq[:, k, h * BANK:(h + 1) * BANK],
                                                start=k == 0, stop=k == KC - 1)
                last.then_inc(ssq_ready, 1)
                yield

            def stage2(i, p):
                pe.wait_ge(fnlo_ready, i + 1)
                pe.wait_ge(fnhi_ready, i + 1)
                wait(pe, masked, i)
                for r in range(NPIX // ROW):
                    n = 0
                    for a, b in PARTS:
                        for k in range(KC):
                            last = nc.tensor.matmul(
                                gram[:, r * ROW:(r + 1) * ROW],
                                fn[p][a][:, k, r * ROW:r * ROW + WINDOW],
                                fn[p][b][:, k, r * ROW:(r + 1) * ROW], start=n == 0, stop=n == 8)
                            n += 1
                last.then_inc(gram_ready, 1)
                yield
                pe.wait_ge(masked, i + 1)
                wait(pe, chi_ready, 2 * i)
                wait(pe, clo_ready, i)
                for h in range(HALVES):
                    for kind in range(KINDS + 1):
                        last = nc.tensor.matmul(corr[0:BACK, h * BANK:(h + 1) * BANK], sel[:, kind, :],
                                                picked[:, kind, h * BANK:(h + 1) * BANK],
                                                start=kind == 0, stop=kind == KINDS)
                last.then_inc(corr_ready, 1)
                yield
                yield
                pe.wait_ge(fhi_ready, i + 1)
                pe.wait_ge(flo_ready, i + 1)
                pe.wait_ge(shifted[p], times16(i, p, NF) + 16 * NF)
                for n in range(EV):
                    j, h = n // HALVES, n % HALVES
                    wait(pe, evicted, EV * i + n - 1)
                    px = slice(h * BANK, (h + 1) * BANK)
                    nc.tensor.matmul(conv[n % 2][:, :], wc[:, j * P:(j + 1) * P], cs[p][:, px],
                                     start=True, stop=False)
                    m = 0
                    for a, b in PARTS:
                        for k in range(KC):
                            last = nc.tensor.matmul(conv[n % 2][:, :], wm[a][:, k, j * P:(j + 1) * P],
                                                    fs[p][b][:, k, px], start=False, stop=m == 8)
                            m += 1
                    last.then_inc(conv_ready, 1)
                yield

            pe.wait_ge(set_up, SETUP)
            pe.wait_ge(c_loaded, 80)
            images(nc.tensor, stage1, stage2)

        @block.vector
        def _(dve):
            nc.vector.memset(ones[:, :], 1.0).then_inc(set_up, 1)
            nc.vector.memset(wc[:, :], 0.0).then_inc(set_up, 1)
            for t in (fn[0][0], fn[0][1], fn[1][0], fn[1][1]):
                last = nc.vector.memset(t[:, :, NPIX:PADDED], 0.0)
            last.then_inc(set_up, 1)
            nc.vector.memset(eps[:, :], EPS).then_inc(set_up, 1)

            def weights():
                dve.wait_ge(w_loaded, 32)
                dve.wait_ge(set_up, 4)
                h, l = (v[:, :, :].rearrange("p k n -> p (k n)") for v in wm)
                nc.vector.tensor_scalar(h, stage_w[:, :], WSCALE, None, ALU.mult).then_inc(set_up, 1)
                nc.vector.tensor_scalar(wc[0:NC + 1, :], stage_c[:, :], WSCALE, None, ALU.mult
                                        ).then_inc(set_up, 1)
                dve.wait_ge(set_up, 6)
                nc.vector.scalar_tensor_tensor(l, stage_w[:, :], WSCALE, h, ALU.mult,
                                               ALU.subtract).then_inc(set_up, 1)
                nc.vector.tensor_copy(wc[CB:CB + NC + 1, :], wc[0:NC + 1, :]).then_inc(set_up, 1)
                nc.vector.scalar_tensor_tensor(wc[2 * CB:2 * CB + NC + 1, :], stage_c[:, :], WSCALE,
                                               wc[0:NC + 1, :], ALU.mult, ALU.subtract
                                               ).then_inc(set_up, 1)

            def stage1(i, p):
                dve.wait_ge(x_loaded[p], times16(i, p) + 16)
                for k in range(KC):
                    for h in range(HALVES):
                        last = nc.vector.bn_stats(bn[:, k, h, :], x[p][:, k, h * BANK:(h + 1) * BANK])
                dve.drain()
                for k in range(KC):
                    last = nc.vector.bn_aggr(mv[:, k, :], bn[:, k, :, :])
                last.then_inc(mv_ready, 1)
                yield
                dve.wait_ge(gmean_ready, i + 1)
                nc.vector.tensor_copy(gm[:, :], stat[:, 0:KC])
                nc.vector.tensor_tensor(dm[:, :], mv[:, :, 0], stat[:, 0:KC], ALU.subtract
                                        ).then_inc(spread, 1)
                dve.wait_ge(spread, 3 * i + 1)
                nc.vector.tensor_tensor(ev[:, :], dm[:, :], dm[:, :], ALU.mult).then_inc(spread, 1)
                dve.wait_ge(spread, 3 * i + 2)
                nc.vector.tensor_tensor(ev[:, :], ev[:, :], mv[:, :, 1], ALU.add).then_inc(spread, 1)
                yield
                dve.wait_ge(gstd_ready, i + 1)
                nc.vector.reciprocal(rs[:, :], rs[:, :]).then_inc(ginv_ready, 1)
                dve.wait_ge(ginv_ready, i + 1)
                wait(dve, fnlo_ready, i)
                wait(dve, fnhi_ready, i)
                for k in range(KC):
                    last = nc.vector.tensor_scalar(f[:, k, :], x[p][:, k, :], gm[:, k:k + 1],
                                                   rs[:, k:k + 1], ALU.subtract, ALU.mult)
                last.then_inc(f_ready, 1)
                yield
                dve.wait_ge(f_ready, i + 1)
                dve.wait_ge(fhi_ready, i + 1)
                nc.vector.tensor_tensor(fs[p][1][:, :, :], f[:, :, :], fs[p][0][:, :, :],
                                        ALU.subtract).then_inc(flo_ready, 1)
                dve.wait_ge(norm_ready, i + 1)
                nc.vector.tensor_scalar(nrm[:, :], nrm[:, :], NORM_EPS, None, ALU.max
                                        ).then_inc(clamped, 1)
                dve.wait_ge(clamped, 2 * i + 1)
                nc.vector.reciprocal(nrm[:, :], nrm[:, :]).then_inc(clamped, 1)
                dve.wait_ge(clamped, 2 * i + 2)
                dve.wait_ge(flo_ready, i + 1)
                dve.wait_ge(squared, i + 1)
                nc.vector.tensor_tensor(f[:, :, :], f[:, :, :],
                                        nrm[:, None, :].broadcast_to([P, KC, NPIX]),
                                        ALU.mult).then_inc(fn_ready, 1)
                yield
                dve.wait_ge(fn_ready, i + 1)
                dve.wait_ge(fnhi_ready, i + 1)
                nc.vector.tensor_tensor(fn[p][1][:, :, 0:NPIX], f[:, :, :], fn[p][0][:, :, 0:NPIX],
                                        ALU.subtract).then_inc(fnlo_ready, 1)
                yield

            def stage2(i, p):
                yield
                dve.wait_ge(gram_ready, i + 1)
                wait(dve, corr_ready, i)
                for kind in range(KINDS + 1):
                    last = nc.vector.tensor_tensor(
                        picked[:, kind, :].rearrange("p (r c) -> p r c", c=ROW),
                        gram[:, :].rearrange("p (r c) -> p r c", c=ROW),
                        mask[:, kind, None, :].broadcast_to([P, NPIX // ROW, ROW]), ALU.mult)
                last.then_inc(masked, 1)
                yield
                dve.wait_ge(chi_ready, 2 * i + 1)
                nc.vector.tensor_tensor(cs[p][CB:CB + BACK, :], corr[0:BACK, :], cs[p][0:BACK, :],
                                        ALU.subtract).then_inc(clo_ready, 1)
                yield
                yield
                if isinstance(i, int):
                    wait(dve, stored[p], times16(i, p))
                else:
                    dve.wait_ge(stored[p], times16(i, p))
                for n in range(EV):
                    j, h = n // HALVES, n % HALVES
                    px = slice(h * BANK, (h + 1) * BANK)
                    dve.wait_ge(conv_ready, EV * i + n + 1)
                    nc.vector.scalar_tensor_tensor(ob[p][:, j, px], conv[n % 2][:, :], 1.0 / WSCALE,
                                                   x[p][:, j, px], ALU.mult, ALU.add
                                                   ).then_inc(evicted, 1)
                yield

            dve.wait_ge(c_loaded, 80)
            weights()
            images(nc.vector, stage1, stage2)

        @block.scalar
        def _(act):
            def stage1(i, p):
                act.wait_ge(gvar_ready, i + 1)
                wait(act, f_ready, i)
                nc.scalar.activation(rs[:, :], stat[:, BANK:BANK + KC], ACT.Sqrt, bias=eps[:, 0:1]
                                     ).then_inc(gstd_ready, 1)
                yield
                act.wait_ge(f_ready, i + 1)
                wait(act, ssq_ready, i)
                nc.scalar.activation(sq[:, :, :], f[:, :, :], ACT.Square).then_inc(squared, 1)
                wait(act, conv_ready, EV * (i - 1))
                nc.scalar.activation(fs[p][0][:, :, :], f[:, :, :], ACT.Copy).then_inc(fhi_ready, 1)
                yield
                act.wait_ge(ssq_ready, i + 1)
                wait(act, fn_ready, i)
                nc.scalar.activation(nrm[:, :], stat[:, :], ACT.Sqrt).then_inc(norm_ready, 1)
                yield
                act.wait_ge(fn_ready, i + 1)
                wait(act, gram_ready, i - 1)
                nc.scalar.activation(fn[p][0][:, :, 0:NPIX], f[:, :, :], ACT.Copy
                                     ).then_inc(fnhi_ready, 1)
                yield

            def stage2(i, p):
                yield
                act.wait_ge(corr_ready, i + 1)
                wait(act, conv_ready, EV * (i - 1))
                nc.scalar.activation(cs[p][0:BACK, :], corr[0:BACK, :], ACT.Copy).then_inc(chi_ready, 1)
                act.wait_ge(chi_ready, 2 * i + 1)
                nc.scalar.activation(cs[p][2 * CB:2 * CB + BACK, :], cs[p][0:BACK, :], ACT.Copy
                                     ).then_inc(chi_ready, 1)
                yield

            act.wait_ge(set_up, 4)
            act.wait_ge(c_loaded, 80)
            images(nc.scalar, stage1, stage2)


def conv_constants():
    import numpy as np

    group = C // 32
    of = np.arange(C) // group
    mean = (of[:, None] == of[None, :]).astype(np.float32) / np.float32(group)
    mean = mean.reshape(KC, P, KC, P).transpose(1, 0, 2, 3).reshape(P, KC * KC, P)
    masks = np.zeros((P, KINDS + 1, ROW), np.float32)
    sel = np.zeros((P, KINDS + 1, BACK), np.float32)
    for dr in range(PAD + 1):
        for q in range(ROW):
            for kind in range(KINDS):
                col = q - forward_column(kind, dr)
                if 0 <= col < ROW:
                    masks[dr * ROW + q, kind, col] = 1
                sel[dr * ROW + q, kind, FORWARD.index((dr, forward_column(kind, dr)))] = 1
            if dr == 0:
                masks[q, KINDS, q] = 1
                sel[q, KINDS, NF:BACK] = 1
    start = np.zeros((3 * CB, NPIX), np.float16)
    start[NC] = 1
    start[2 * CB + NC] = 1
    return {"group_mean": np.ascontiguousarray(mean), "masks": masks, "selectors": sel, "corr_start": start}


def corr_weight_rows():
    left = list(enumerate(REFERENCE_SHIFTS))
    rows = []
    for shift in CORR_ROWS:
        at = next(n for n, (_, s) in enumerate(left) if s == shift)
        rows.append(left.pop(at)[0])
    return rows


def attention_stage(nc, x_in, w_q, w_k, w_v, w_o, b_o, identity, out, n_images):
    HEAD = 32
    HG = P // HEAD
    GROUPS = KC
    STEPS = HG
    SCORES = 2 * STEPS
    NST = 3
    UNITS = 8
    IU = UNITS * GROUPS
    TILES = NPIX // P
    ITEMS = HG * TILES * HALVES
    MAXROW = 3 * HEAD
    SCALE = HEAD ** -0.5
    EPS = 1e-5
    QUARTER = BANK // 4
    NQKV = 6 * GROUPS
    FIRST = 6
    STACKED = 16 * (6 * HG + 1)
    ctx = ExitStack()
    with ctx:
        N = Names(nc, ctx, "b")
        ws = [[N.sb(f"w{n}{s}", [P, KC, C], F16) for s in range(2)] for n in "qkvo"]
        bo = N.sb("bo", [P, KC])
        ident = N.sb("ident", [P, P])
        mean_w = N.sb("mean_w", [P, P])
        ones = N.sb("ones", [P, HEAD])
        eps = N.sb("eps", [P, 1])
        xl = N.sb("xl", [P, KC, NPIX])
        std = [N.sb(f"std{h}", [P, BANK]) for h in range(HALVES)]
        z = [N.sb(f"z{s}", [P, KC, NPIX], F16) for s in range(2)]
        sq = z[1][:, :, :].rearrange("p k n -> p (k n)").bitcast(F32).rearrange(
            "p (k n) -> p k n", k=KC)
        staged = [[[N.sb(f"staged{e}{n}{s}", [P, NPIX], F16) for s in range(2)] for n in "qk"]
                  for e in range(2)]
        vstaged = N.sb("vstaged", [P, TILES, P])
        qst = [N.sb(f"qst{g}", [P, HG, NPIX], F16) for g in range(GROUPS)]
        kst = [N.sb(f"kst{g}", [P, HG, NPIX], F16) for g in range(GROUPS)]
        v = [N.sb(f"v{g}", [P, TILES, P]) for g in range(GROUPS)]
        mxp = [N.sb(f"mxp{e}", [P, TILES, HALVES]) for e in range(2)]
        nm = [N.sb(f"nm{e}", [P, TILES]) for e in range(2)]
        mr = [N.sb(f"mr{e}", [TILES, P], F16) for e in range(2)]
        ex = [N.sb(f"ex{k}", [P, NPIX]) for k in range(2 * HG)]
        pair = [N.sb(f"pair{k}", [P, BANK]) for k in range(2 * HG)]
        pvs = N.sb("pvs", [P, BANK])
        inv = N.sb("inv", [P, BANK])
        ao = [N.sb(f"ao{s}", [P, KC, NPIX], F16) for s in range(2)]
        ot = N.sb("ot", [P, BANK])
        xr = N.sb("xr", [P, KC, NPIX])
        stage_w = xr[:, :, :].rearrange("p k n -> p (k n)")[:, 0:KC * C]
        st = [N.ps(f"st{e}", [P, BANK]) for e in range(NST)]
        mx = [N.ps(f"mx{e}", [P, BANK]) for e in range(2)]
        pj = N.ps("pj", [P, BANK])
        pv = N.ps("pv", [P, BANK])
        sm = N.ps("sm", [P, BANK])

        w_loaded = N.sem("w_loaded")
        w_split = N.sem("w_split")
        c_loaded = N.sem("c_loaded")
        const_set = N.sem("const_set")
        x_loaded = N.sem("x_loaded")
        mean_ready = N.sem("mean_ready")
        centred = N.sem("centred")
        squared = N.sem("squared")
        var_ready = N.sem("var_ready")
        std_ready = N.sem("std_ready")
        inv_ready = N.sem("inv_ready")
        z_ready = N.sem("z_ready")
        zhi_ready = N.sem("zhi_ready")
        zlo_ready = N.sem("zlo_ready")
        proj_ready = N.sem("proj_ready")
        hi_staged = N.sem("hi_staged")
        lo_staged = N.sem("lo_staged")
        v_staged = N.sem("v_staged")
        stacked = [N.sem(f"stacked{g}") for g in range(GROUPS)]
        mx_ready = N.sem("mx_ready")
        mx_taken = N.sem("mx_taken")
        combined = N.sem("combined")
        turned = N.sem("turned")
        row_ready = N.sem("row_ready")
        row_loaded = [N.sem(f"row_loaded{h}") for h in range(HG)]
        st_ready = N.sem("st_ready")
        exp_ready = N.sem("exp_ready")
        pair_ready = N.sem("pair_ready")
        pv_ready = N.sem("pv_ready")
        sum_ready = N.sem("sum_ready")
        pv_moved = N.sem("pv_moved")
        sum_inverted = N.sem("sum_inverted")
        att_ready = N.sem("att_ready")
        ahi_ready = N.sem("ahi_ready")
        alo_ready = N.sem("alo_ready")
        o_ready = N.sem("o_ready")
        o_moved = N.sem("o_moved")
        o_added = N.sem("o_added")
        r_loaded = N.sem("r_loaded")
        stored = N.sem("stored")
        block = ctx.enter_context(nc.Block())

        def schedule(eng, prologue, unit, epilogue):
            last = n_images - 1
            prologue()
            for u in range(FIRST):
                unit(0, u, out_proj=False, norm=True)
            with eng.Fori(0, last - 1) as b:
                for u in range(FIRST, IU):
                    unit(b, u)
                for u in range(FIRST):
                    unit(b + 1, u)
            for u in range(FIRST, IU):
                unit(last - 1, u)
            for u in range(FIRST):
                unit(last, u, norm=False)
            for u in range(FIRST, IU):
                unit(last, u, norm=False, qkv=False, maxima=u < IU - UNITS)
            epilogue(last)

        def turn_of(b, u):
            return HG * (GROUPS * b + u // UNITS + 1) + (u % UNITS) // 2 - 1

        @block.sync
        def _(sp):
            def load_x(m):
                wait(sp, zlo_ready, 2 * m)
                sp.dma_start(xl[:, :, :], image_tile(x_in, m)).then_inc(x_loaded, 16)

            def load_r(b):
                wait(sp, stored, 16 * b)
                sp.dma_start(xr[:, :, :], image_tile(x_in, b)).then_inc(r_loaded, 16)

            def stack(m, g):
                e = g % 2
                wait_both(sp, (lo_staged, 12 * m + 4 * g + 4), (v_staged, 6 * m + 2 * g + 2))
                wait(sp, pv_ready, 2 * (IU * (m - 1) + UNITS * (g + 1)))
                for dst, part, (a, b, c) in ((qst, 0, (0, 1, 0)), (kst, 1, (0, 0, 1))):
                    for r, s in enumerate((a, b, c)):
                        for h in range(HG):
                            sp.dma_start(dst[g][r * HEAD:(r + 1) * HEAD, h, :],
                                         staged[e][part][s][h * HEAD:(h + 1) * HEAD, :]
                                         ).then_inc(stacked[g], 16)
                sp.dma_start(v[g][:, :, :], vstaged[:, :, :]).then_inc(stacked[g], 16)

            def load_row(turn, g, h):
                sp.wait_ge(row_ready, turn + 1)
                sp.dma_start(qst[g][MAXROW:MAXROW + 1, h, :], mr[h % 2][:, :]).then_inc(row_loaded[h], 16)

            def prologue():
                for n, w in enumerate((w_q, w_k, w_v, w_o)):
                    if n:
                        sp.wait_ge(w_split, 2 * n)
                    sp.dma_start(stage_w.rearrange("p (k n) -> p k n", k=KC),
                                 w.rearrange("(k p) n -> p k n", p=P)).then_inc(w_loaded, 16)
                    if n == 0:
                        load_x(0)
                        sp.dma_start(ident[:, :], identity).then_inc(c_loaded, 16)
                        sp.dma_start(bo[:, :], b_o).then_inc(c_loaded, 16)
                sp.wait_ge(w_split, 8)
                load_r(0)
                load_x(1)
                for g in range(GROUPS):
                    stack(0, g)
                for h in range(HG - 1):
                    load_row(h, 0, h)

            def unit(b, u, qkv=True, maxima=True):
                g, w = u // UNITS, u % UNITS
                if w == 0:
                    load_row(turn_of(b, u), g, HG - 1)
                elif w % 2 == 0 and maxima:
                    load_row(turn_of(b, u), (g + 1) % GROUPS, w // 2 - 1)
                if u == 0 and not (isinstance(b, int) and b == 0):
                    stack(b, 2)
                if u == 12 and qkv:
                    stack(b + 1, 0)
                if u == 18 and qkv:
                    stack(b + 1, 1)

            def epilogue(b):
                sp.wait_ge(o_added, 6 * (b + 1))
                sp.dma_start(image_tile(out, b), xr[:, :, :]).then_inc(stored, 16)
                sp.wait_ge(stored, 16 * (b + 1))

            last = n_images - 1
            prologue()
            for u in range(FIRST):
                unit(0, u)
            with sp.Fori(0, last - 1) as b:
                for u in range(FIRST, IU):
                    unit(b, u)
                    if u == FIRST:
                        load_x(b + 2)
                for u in range(FIRST):
                    unit(b + 1, u)
                sp.wait_ge(o_added, 6 * b + 6)
                sp.dma_start(image_tile(out, b), xr[:, :, :]).then_inc(stored, 16)
                load_r(b + 1)
            for u in range(FIRST, IU):
                unit(last - 1, u)
            for u in range(FIRST):
                unit(last, u)
            sp.wait_ge(o_added, 6 * last)
            sp.dma_start(image_tile(out, last - 1), xr[:, :, :]).then_inc(stored, 16)
            load_r(last)
            for u in range(FIRST, IU):
                unit(last, u, qkv=False, maxima=u < IU - UNITS)
            epilogue(last)

        @block.tensor
        def _(pe):
            free = []

            def take_pj(*released_by):
                for s, value in free:
                    wait(pe, s, value)
                free[:] = released_by

            def mean(m, h):
                take_pj((centred, 2 * m + h + 1))
                pe.wait_ge(x_loaded, 16 * (m + 1))
                for k in range(KC):
                    last = nc.tensor.matmul(pj[:, :], mean_w[:, :], xl[:, k, h * BANK:(h + 1) * BANK],
                                            start=k == 0, stop=k == KC - 1)
                last.then_inc(mean_ready, 1)

            def var(m, h):
                take_pj((std_ready, 2 * m + h + 1))
                pe.wait_ge(squared, 2 * m + h + 1)
                for k in range(KC):
                    last = nc.tensor.matmul(pj[:, :], mean_w[:, :], sq[:, k, :],
                                            start=k == 0, stop=k == KC - 1)
                last.then_inc(var_ready, 1)

            def project(m, i):
                g, kind, part = i // 6, (i % 6) // 2, i % 2
                if kind < 2:
                    take_pj((lo_staged, 12 * m + 4 * g + 2 * kind + part + 1))
                    pe.wait_ge(zhi_ready, 2 * m + part + 1)
                    pe.wait_ge(zlo_ready, 2 * m + part + 1)
                else:
                    take_pj((v_staged, 6 * m + 2 * g + part + 1))
                    pe.wait_ge(zhi_ready, 2 * m + 2)
                    pe.wait_ge(zlo_ready, 2 * m + 2)

            def project_part(m, i, n0, n1):
                g, kind, part = i // 6, (i % 6) // 2, i % 2
                last = None
                if kind < 2:
                    for n in range(n0, n1):
                        (a, b), k = PARTS[n // KC], n % KC
                        last = nc.tensor.matmul(pj[:, :], ws[kind][a][:, k, g * P:(g + 1) * P],
                                                z[b][:, k, part * BANK:(part + 1) * BANK],
                                                start=n == 0, stop=n == 8)
                else:
                    tiles = range(*{(0, 5): (0, 2), (5, 9): (2, 4), (0, 9): (0, 4)}[n0, n1])
                    for t in tiles:
                        at = (part * 4 + t) * P
                        for n in range(9):
                            (a, b), k = PARTS[n // KC], n % KC
                            last = nc.tensor.matmul(pj[:, t * P:(t + 1) * P], z[a][:, k, at:at + P],
                                                    ws[2][b][:, k, g * P:(g + 1) * P],
                                                    start=n == 0, stop=n == 8)
                if n1 == 9:
                    last.then_inc(proj_ready, 1)

            def out_project(b, i):
                h, j = i // KC, i % KC
                take_pj((o_moved, 6 * b + i + 1))
                pe.wait_ge(ahi_ready, 6 * b + 4 + h + 1)
                pe.wait_ge(alo_ready, 6 * b + 4 + h + 1)
                for n in range(9):
                    (a, c), k = PARTS[n // KC], n % KC
                    last = nc.tensor.matmul(pj[:, :], ws[3][a][:, k, j * P:(j + 1) * P],
                                            ao[c][:, k, h * BANK:(h + 1) * BANK],
                                            start=n == 0, stop=n == 8)
                last.then_inc(o_ready, 1)

            def scores(b, u, s):
                g, w = u // UNITS, u % UNITS
                half, kp = w // 4, w % 4
                if w == 0:
                    pe.wait_ge(row_loaded[s], 16 * (GROUPS * b + g + 1))
                for e in range(2):
                    kt = 2 * kp + e
                    n = 2 * s + e
                    wait(pe, exp_ready, SCORES * (IU * b + u) + n + 1 - NST)
                    nc.tensor.matmul(st[(SCORES * u + n) % NST][:, :],
                                     kst[g][0:MAXROW + 1, s, kt * P:(kt + 1) * P],
                                     qst[g][0:MAXROW + 1, s, half * BANK:(half + 1) * BANK],
                                     start=True, stop=True).then_inc(st_ready, 1)

            def max_scores(group, m, g, item):
                h, t, half = item // (2 * TILES), item // 2 % TILES, item % 2
                wait(pe, mx_taken, ITEMS * group + item - 1)
                if item % (2 * TILES) == 1:
                    wait(pe, row_ready, HG * group + h)
                if item == 0:
                    pe.wait_ge(stacked[g], STACKED * (m + 1))
                nc.tensor.matmul(mx[item % 2][:, :], qst[g][0:MAXROW, h, t * P:(t + 1) * P],
                                 kst[g][0:MAXROW, h, half * BANK:(half + 1) * BANK],
                                 start=True, stop=True).then_inc(mx_ready, 1)

            def turn(number, parity):
                pe.wait_ge(combined, number + 1)
                nc.tensor.transpose(mx[1][0:TILES, 0:P], nm[parity][:, :], ident[:, :]).then_inc(turned, 1)

            def weigh(b, u, e):
                g, w = u // UNITS, u % UNITS
                unit_no = IU * b + u
                kt = 2 * (w % 4) + e
                if e == 0:
                    pe.wait_ge(exp_ready, SCORES * (unit_no + 1))
                    if w % 4 == 0:
                        wait(pe, pv_moved, 6 * b + u // 4)
                        if w == 0:
                            pe.wait_ge(stacked[g], STACKED * (b + 1))
                for h in range(HG):
                    last = nc.tensor.matmul(pv[h * HEAD:(h + 1) * HEAD, :],
                                            v[g][:, kt, h * HEAD:(h + 1) * HEAD],
                                            ex[u % 2 * HG + h][:, e * BANK:(e + 1) * BANK],
                                            start=kt == 0, stop=kt == TILES - 1,
                                            tile_position=(0, h * HEAD))
                last.then_inc(pv_ready, 1)

            def sum_up(b, u):
                w = u % UNITS
                unit_no = IU * b + u
                pe.wait_ge(pair_ready, STEPS * unit_no + STEPS)
                if w % 4 == 0:
                    wait(pe, sum_inverted, 4 * (6 * b + u // 4))
                for h in range(HG):
                    last = nc.tensor.matmul(sm[h * HEAD:(h + 1) * HEAD, :], ones[:, :],
                                            pair[u % 2 * HG + h][:, :], start=w % 4 == 0,
                                            stop=w % 4 == 3, tile_position=(0, h * HEAD))
                last.then_inc(sum_ready, 1)

            def prologue():
                pe.wait_ge(const_set, 3)
                for h in range(HALVES):
                    mean(0, h)
                for h in range(HALVES):
                    var(0, h)
                pe.wait_ge(w_split, 6)
                for i in range(NQKV):
                    project(0, i)
                    project_part(0, i, 0, 9)
                pe.wait_ge(c_loaded, 32)
                for h in range(HG):
                    for item in range(2 * TILES * h, 2 * TILES * (h + 1)):
                        max_scores(0, 0, 0, item)
                    if h < HG - 1:
                        turn(h, h % 2)

            def unit(b, u, out_proj=True, norm=True, qkv=True, maxima=True):
                g, w = u // UNITS, u % UNITS
                group = GROUPS * b + g + 1
                image = b + 1 if g == GROUPS - 1 else b
                lag = (b, u - 1) if u else (b - 1, IU - 1)
                lagging = not (isinstance(b, int) and b == 0 and u == 0)
                if u == FIRST and qkv:
                    free[:] = [(std_ready, 2 * b + 4)]

                def maximum(s, e):
                    if maxima:
                        max_scores(group, image, (g + 1) % GROUPS, 8 * w + 2 * s + e)

                scores(b, u, 0)
                if u >= FIRST and qkv:
                    project(b + 1, u - FIRST)
                    project_part(b + 1, u - FIRST, 0, 5)
                if u < FIRST and out_proj:
                    out_project(b - 1, u)
                maximum(0, 0)
                if u >= FIRST and qkv:
                    project_part(b + 1, u - FIRST, 5, 9)
                if w == 0 or w % 2 == 0 and maxima:
                    turn(turn_of(b, u), turn_of(0, u) % 2)
                scores(b, u, 1)
                maximum(0, 1)
                if lagging:
                    weigh(*lag, 0)
                maximum(1, 0)
                scores(b, u, 2)
                maximum(1, 1)
                if lagging:
                    weigh(*lag, 1)
                maximum(2, 0)
                if norm and u < 4:
                    (mean if u < 2 else var)(b + 1, u % 2)
                scores(b, u, 3)
                maximum(2, 1)
                if lagging:
                    sum_up(*lag)
                maximum(3, 0)
                maximum(3, 1)

            def epilogue(b):
                weigh(b, IU - 1, 0)
                weigh(b, IU - 1, 1)
                sum_up(b, IU - 1)
                for i in range(6):
                    out_project(b, i)

            schedule(nc.tensor, prologue, unit, epilogue)

        @block.vector
        def _(dve):
            def half_of(t, h):
                return t[:, :, h * BANK:(h + 1) * BANK]

            def centre(m, h):
                dve.wait_ge(mean_ready, 2 * m + h + 1)
                nc.vector.tensor_tensor(half_of(xl, h), half_of(xl, h),
                                        pj[:, None, :].broadcast_to([P, KC, BANK]),
                                        ALU.subtract).then_inc(centred, 1)

            def invert_std(m, h, quarter):
                at = slice(quarter * QUARTER, (quarter + 1) * QUARTER)
                dve.wait_ge(std_ready, 2 * m + h + 1)
                nc.vector.reciprocal(std[h][:, at], std[h][:, at]).then_inc(inv_ready, 1)

            def normalise(m, h, k):
                at = slice(h * BANK, (h + 1) * BANK)
                dve.wait_ge(inv_ready, 8 * m + 4 * h + 4)
                dve.wait_ge(squared, 2 * m + h + 1)
                nc.vector.tensor_tensor(xl[:, k, at], xl[:, k, at], std[h][:, :], ALU.mult
                                        ).then_inc(z_ready, 1)

            def z_low(m, h, k):
                at = slice(h * BANK, (h + 1) * BANK)
                dve.wait_ge(zhi_ready, 2 * m + h + 1)
                ins = nc.vector.tensor_tensor(z[1][:, k, at], xl[:, k, at], z[0][:, k, at],
                                              ALU.subtract)
                if k == KC - 1:
                    ins.then_inc(zlo_ready, 1)

            def stage_low(m, i):
                g, kind, part = i // 6, (i % 6) // 2, i % 2
                if kind == 2:
                    return
                dve.wait_ge(hi_staged, 12 * m + 4 * g + 2 * kind + part + 1)
                hi, lo = staged[g % 2][kind]
                at = slice(part * BANK, (part + 1) * BANK)
                nc.vector.scalar_tensor_tensor(lo[:, at], pj[:, :], 1.0 / WSCALE, hi[:, at],
                                               ALU.mult, ALU.subtract).then_inc(lo_staged, 1)

            def take_max(group, item):
                h, t, half = item // (2 * TILES), item // 2 % TILES, item % 2
                dve.wait_ge(mx_ready, ITEMS * group + item + 1)
                nc.vector.reduce_max(mxp[h % 2][:, t, half:half + 1], mx[item % 2][:, :], AX_X
                                     ).then_inc(mx_taken, 1)

            def combine(number, parity):
                dve.wait_ge(mx_taken, 2 * TILES * (number + 1))
                wait(dve, turned, number - 1)
                nc.vector.reduce_max(nm[parity][:, :], mxp[parity][:, :, :], AX_X
                                     ).then_inc(combined, 1)

            def invert_sum(b, x, quarter):
                at = slice(quarter * QUARTER, (quarter + 1) * QUARTER)
                dve.wait_ge(sum_ready, 4 * (6 * b + x + 1))
                wait(dve, att_ready, 6 * b + x)
                nc.vector.reciprocal(inv[:, at], sm[:, at]).then_inc(sum_inverted, 1)

            def attended(b, x):
                dve.wait_ge(sum_inverted, 4 * (6 * b + x + 1))
                dve.wait_ge(pv_moved, 6 * b + x + 1)
                nc.vector.tensor_tensor(pvs[:, :], pvs[:, :], inv[:, :], ALU.mult
                                        ).then_inc(att_ready, 1)

            def prologue():
                nc.vector.memset(mean_w[:, :], 1.0 / C)
                nc.vector.memset(ones[:, :], 1.0).then_inc(const_set, 1)
                nc.vector.memset(eps[:, :], EPS).then_inc(const_set, 1)
                for g in range(GROUPS):
                    last = nc.vector.memset(kst[g][MAXROW:MAXROW + 1, :, :], 1.0)
                last.then_inc(const_set, 1)

                def split(n):
                    dve.wait_ge(w_loaded, 16 * (n + 1))
                    h, l = (t[:, :, :].rearrange("p k n -> p (k n)") for t in ws[n])
                    nc.vector.tensor_scalar(h, stage_w, WSCALE, None, ALU.mult
                                            ).then_inc(w_split, 1)
                    dve.wait_ge(w_split, 2 * n + 1)
                    nc.vector.scalar_tensor_tensor(l, stage_w, WSCALE, h, ALU.mult,
                                                   ALU.subtract).then_inc(w_split, 1)

                split(0)
                for h in range(HALVES):
                    centre(0, h)
                split(1)
                split(2)
                split(3)
                for h in range(HALVES):
                    for quarter in range(4):
                        invert_std(0, h, quarter)
                    for k in range(KC):
                        normalise(0, h, k)
                    for k in range(KC):
                        z_low(0, h, k)
                for i in range(NQKV):
                    stage_low(0, i)
                for h in range(HG):
                    for item in range(2 * TILES * h, 2 * TILES * (h + 1)):
                        take_max(0, item)
                    if h < HG - 1:
                        combine(h, h % 2)

            def unit(b, u, out_proj=True, norm=True, qkv=True, maxima=True):
                g, w = u // UNITS, u % UNITS
                group = GROUPS * b + g + 1
                started = not (isinstance(b, int) and b == 0 and u < 4)

                def maximum(s, e):
                    if maxima:
                        take_max(group, 8 * w + 2 * s + e)

                def gap(s):
                    if started and u % 4 == 0 and s == 3:
                        invert_sum(b, (u - 4) // 4, 0)
                        invert_sum(b, (u - 4) // 4, 1)
                    if started and u % 4 == 1:
                        if s < 2:
                            invert_sum(b, (u - 5) // 4, s + 2)
                        elif s == 2:
                            attended(b, (u - 5) // 4)
                    if norm and s < 3 and u == 5:
                        z_low(b + 1, 0, s)
                    if norm and s < 3 and u == 6:
                        z_low(b + 1, 1, s)
                    if norm and s > 0 and u == 4:
                        normalise(b + 1, 0, s - 1)
                    if norm and s < 3 and u == 5:
                        normalise(b + 1, 1, s)
                    if norm and u in (3, 4) and s < 4:
                        invert_std(b + 1, u - 3, s)

                if w == 0 or w % 2 == 0 and maxima:
                    combine(turn_of(b, u), turn_of(0, u) % 2)
                gap(0)
                maximum(0, 0)
                maximum(0, 1)
                if u >= FIRST and qkv:
                    stage_low(b + 1, u - FIRST)
                maximum(1, 0)
                gap(1)
                maximum(1, 1)
                maximum(2, 0)
                gap(2)
                if norm and u < 2:
                    centre(b + 1, u)
                maximum(2, 1)
                maximum(3, 0)
                maximum(3, 1)
                gap(3)

            def epilogue(b):
                for quarter in range(4):
                    invert_sum(b, 5, quarter)
                attended(b, 5)

            schedule(nc.vector, prologue, unit, epilogue)

        @block.scalar
        def _(act):
            def square(m, h):
                act.wait_ge(centred, 2 * m + h + 1)
                wait(act, var_ready, 2 * m + h)
                wait(act, proj_ready, NQKV * m)
                nc.scalar.activation(sq[:, :, :], xl[:, :, h * BANK:(h + 1) * BANK], ACT.Square
                                     ).then_inc(squared, 1)

            def root(m, h):
                act.wait_ge(var_ready, 2 * m + h + 1)
                wait(act, z_ready, 6 * (m - 1) + 3 * h + 3)
                nc.scalar.activation(std[h][:, :], pj[:, :], ACT.Sqrt, bias=eps[:, 0:1]
                                     ).then_inc(std_ready, 1)

            def z_high(m, h):
                act.wait_ge(z_ready, 6 * m + 3 * h + 3)
                wait(act, proj_ready, NQKV * m)
                at = slice(h * BANK, (h + 1) * BANK)
                nc.scalar.activation(z[0][:, :, at], xl[:, :, at], ACT.Copy).then_inc(zhi_ready, 1)

            def stage_high(m, i):
                g, kind, part = i // 6, (i % 6) // 2, i % 2
                act.wait_ge(proj_ready, NQKV * m + i + 1)
                if i % 6 == 0:
                    if g == 2:
                        act.wait_ge(stacked[0], STACKED * (m + 1))
                    else:
                        wait(act, stacked[2 if g == 0 else 1], STACKED * m)
                if i % 6 == 4:
                    if g == 0:
                        wait(act, stacked[2], STACKED * m)
                    else:
                        act.wait_ge(stacked[g - 1], STACKED * (m + 1))
                if kind == 2:
                    nc.scalar.activation(vstaged[:, 4 * part:4 * part + 4, :],
                                         pj[:, :].rearrange("p (t n) -> p t n", n=P), ACT.Copy,
                                         scale=1.0 / WSCALE).then_inc(v_staged, 1)
                else:
                    at = slice(part * BANK, (part + 1) * BANK)
                    nc.scalar.activation(staged[g % 2][kind][0][:, at], pj[:, :], ACT.Copy,
                                         scale=1.0 / WSCALE).then_inc(hi_staged, 1)

            def row(number, h):
                act.wait_ge(turned, number + 1)
                if h >= 2:
                    act.wait_ge(row_loaded[h - 2], 4 * (number - h) + 16)
                else:
                    wait(act, row_loaded[h + 2], 4 * (number - h))
                nc.scalar.activation(mr[h % 2][:, :], mx[1][0:TILES, 0:P], ACT.Copy, scale=-1.0
                                     ).then_inc(row_ready, 1)

            def exponentials(b, u, s):
                unit_no = IU * b + u
                if not (isinstance(b, int) and b == 0 and u < 2):
                    act.wait_ge(pv_ready, 2 * unit_no - 2)
                    act.wait_ge(pair_ready, STEPS * unit_no + s - 2 * STEPS + 1)
                for e in range(2):
                    n = 2 * s + e
                    act.wait_ge(st_ready, SCORES * unit_no + n + 1)
                    nc.scalar.activation(ex[u % 2 * HG + s][:, e * BANK:(e + 1) * BANK],
                                         st[(SCORES * u + n) % NST][:, :], ACT.Exp,
                                         scale=SCALE).then_inc(exp_ready, 1)

            def move_pv(b, x):
                act.wait_ge(pv_ready, 8 * (6 * b + x + 1))
                wait(act, alo_ready, 6 * b + x)
                wait(act, ahi_ready, 6 * b + x)
                nc.scalar.activation(pvs[:, :], pv[:, :], ACT.Copy).then_inc(pv_moved, 1)

            def attended_high(b, x):
                g, h = x // 2 % GROUPS, x % 2
                act.wait_ge(att_ready, 6 * b + x + 1)
                nc.scalar.activation(ao[0][:, g, h * BANK:(h + 1) * BANK], pvs[:, :], ACT.Copy
                                     ).then_inc(ahi_ready, 1)

            def move_out(b, i):
                act.wait_ge(o_ready, 6 * b + i + 1)
                if i:
                    act.wait_ge(o_added, 6 * b + i)
                nc.scalar.activation(ot[:, :], pj[:, :], ACT.Identity, bias=bo[:, i % KC:i % KC + 1],
                                     scale=1.0 / WSCALE).then_inc(o_moved, 1)

            def prologue():
                act.wait_ge(const_set, 3)
                act.wait_ge(c_loaded, 32)
                for h in range(HALVES):
                    square(0, h)
                    root(0, h)
                for h in range(HALVES):
                    z_high(0, h)
                for i in range(NQKV):
                    stage_high(0, i)
                for h in range(HG - 1):
                    row(h, h)

            def unit(b, u, out_proj=True, norm=True, qkv=True, maxima=True):
                w = u % UNITS
                started = not (isinstance(b, int) and b == 0 and u < 4)
                exponentials(b, u, 0)
                if w == 0:
                    row(turn_of(b, u), HG - 1)
                elif w % 2 == 0 and maxima:
                    row(turn_of(b, u), w // 2 - 1)
                if started and u % 4 == 2:
                    attended_high(b, (u - 6) // 4)
                if norm and u == 1:
                    square(b + 1, 0)
                if norm and u == 5:
                    z_high(b + 1, 0)
                exponentials(b, u, 1)
                if u >= FIRST and qkv:
                    stage_high(b + 1, u - FIRST)
                if u < FIRST and out_proj:
                    move_out(b - 1, u)
                exponentials(b, u, 2)
                if norm and u in (2, 3):
                    root(b + 1, u - 2)
                exponentials(b, u, 3)
                if started and u % 4 == 0:
                    move_pv(b, (u - 4) // 4)
                if norm and u == 2:
                    square(b + 1, 1)
                if norm and u == 5:
                    z_high(b + 1, 1)

            def epilogue(b):
                move_pv(b, 5)
                attended_high(b, 5)
                for i in range(6):
                    move_out(b, i)

            schedule(nc.scalar, prologue, unit, epilogue)

        @block.gpsimd
        def _(pool):
            def attended_low(b, x):
                g, h = x // 2 % GROUPS, x % 2
                at = slice(h * BANK, (h + 1) * BANK)
                pool.wait_ge(att_ready, 6 * b + x + 1)
                pool.wait_ge(ahi_ready, 6 * b + x + 1)
                nc.gpsimd.tensor_tensor(ao[1][:, g, at], pvs[:, :], ao[0][:, g, at], ALU.subtract
                                        ).then_inc(alo_ready, 1)

            def add(b, i):
                h, j = i // KC, i % KC
                at = slice(h * BANK, (h + 1) * BANK)
                pool.wait_ge(o_moved, 6 * b + i + 1)
                if i == 0:
                    pool.wait_ge(r_loaded, 16 * (b + 1))
                nc.gpsimd.tensor_tensor(xr[:, j, at], xr[:, j, at], ot[:, :], ALU.add
                                        ).then_inc(o_added, 1)

            def unit(b, u, out_proj=True, **_flags):
                unit_no = IU * b + u
                started = not (isinstance(b, int) and b == 0 and u < 4)
                for s in range(STEPS):
                    if started and u % 4 == 2 and s == 1:
                        attended_low(b, (u - 6) // 4)
                    if u < FIRST and out_proj and s == 2:
                        add(b - 1, u)
                    pool.wait_ge(exp_ready, SCORES * unit_no + 2 * s + 2)
                    wait(pool, sum_ready, unit_no - 1)
                    e = ex[u % 2 * HG + s]
                    nc.gpsimd.tensor_tensor(pair[u % 2 * HG + s][:, :], e[:, 0:BANK], e[:, BANK:NPIX],
                                            ALU.add).then_inc(pair_ready, 1)

            def epilogue(b):
                attended_low(b, 5)
                for i in range(6):
                    add(b, i)

            schedule(nc.gpsimd, lambda: None, unit, epilogue)


def ffn_stage(nc, x_in, w_in, b_in, w_out, out, n_images):
    HID = w_in.shape[1]
    MC = HID // P
    LAG = 2
    NH, NG, NS = 3, 3, 4
    EPS = 1e-5
    ctx = ExitStack()
    with ctx:
        N = Names(nc, ctx, "c")
        stage_w = N.sb("stage_w", [P, KC * HID])
        wi = [N.sb(f"wi{s}", [P, KC, HID], F16) for s in range(2)]
        wo = [N.sb(f"wo{s}", [P, MC, C], F16) for s in range(2)]
        bias = N.sb("bias", [P, MC])
        mean_w = N.sb("mean_w", [P, P])
        eps = N.sb("eps", [P, 1])
        x = [N.sb(f"x{p}", [P, KC, BANK]) for p in range(2)]
        d = N.sb("d", [P, KC, BANK])
        sq = N.sb("sq", [P, KC, BANK])
        std = N.sb("std", [P, BANK])
        z = [[N.sb(f"z{p}{s}", [P, KC, BANK], F16) for s in range(2)] for p in range(2)]
        g = [N.sb(f"g{k}", [P, BANK]) for k in range(NG)]
        gs = [[N.sb(f"gs{k}{s}", [P, BANK], F16) for s in range(2)] for k in range(NS)]
        ob = [N.sb(f"ob{p}", [P, KC, BANK]) for p in range(2)]
        hid = [N.ps(f"hid{k}", [P, BANK]) for k in range(NH)]
        acc = [N.ps(f"acc{k}", [P, BANK]) for k in range(KC)]
        stat = [N.ps(f"stat{k}", [P, BANK]) for k in range(2)]

        w_loaded = N.sem("w_loaded")
        w_split = N.sem("w_split")
        const_set = N.sem("const_set")
        x_loaded = [N.sem(f"x_loaded{p}") for p in range(2)]
        stored = [N.sem(f"stored{p}") for p in range(2)]
        mean_ready = N.sem("mean_ready")
        centred = N.sem("centred")
        squared = N.sem("squared")
        var_ready = N.sem("var_ready")
        std_ready = N.sem("std_ready")
        inv_ready = N.sem("inv_ready")
        z_ready = N.sem("z_ready")
        zhi_ready = N.sem("zhi_ready")
        zlo_ready = N.sem("zlo_ready")
        hid_ready = N.sem("hid_ready")
        gelu_ready = N.sem("gelu_ready")
        ghi_ready = N.sem("ghi_ready")
        glo_ready = N.sem("glo_ready")
        out_used = N.sem("out_used")
        evicted = N.sem("evicted")
        block = ctx.enter_context(nc.Block())

        T = 2 * n_images

        def tiles(eng, body):
            body(0, 0, True, False)
            body(1, 1, False, False)
            body(2, 0, False, False)
            with eng.Fori(1, n_images - 1) as image:
                body(2 * image + 1, 1, False, False)
                body(2 * image + 2, 0, False, False)
            body(T - 1, 1, False, True)

        @block.sync
        def _(sp):
            sp.dma_start(stage_w[:, :].rearrange("p (k n) -> p k n", k=KC),
                         w_in.rearrange("(k p) n -> p k n", p=P)).then_inc(w_loaded, 16)
            sp.dma_start(bias[:, :], b_in).then_inc(w_loaded, 16)
            sp.dma_start(x[0][:, :, :], image_tile(x_in, 0, 0, BANK)).then_inc(x_loaded[0], 16)
            sp.wait_ge(w_split, 2)
            sp.dma_start(stage_w[:, :].rearrange("p (k n) -> p k n", k=MC),
                         w_out.rearrange("(k p) n -> p k n", p=P)).then_inc(w_loaded, 16)
            sp.dma_start(x[1][:, :, :], image_tile(x_in, 0, BANK, BANK)).then_inc(x_loaded[1], 16)

            def turn(image, p, load):
                sp.wait_ge(evicted, KC * (2 * image + p + 1))
                if load:
                    sp.dma_start(x[p][:, :, :], image_tile(x_in, image + 1, BANK * p, BANK)
                                 ).then_inc(x_loaded[p], 16)
                sp.dma_start(image_tile(out, image, BANK * p, BANK), ob[p][:, :, :]
                             ).then_inc(stored[p], 16)

            with sp.Fori(0, n_images - 1) as image:
                turn(image, 0, True)
                turn(image, 1, True)
            turn(n_images - 1, 0, False)
            turn(n_images - 1, 1, False)
            for p in range(2):
                sp.wait_ge(stored[p], 16 * n_images)

        @block.tensor
        def _(pe):
            def mean(t, p):
                pe.wait_ge(x_loaded[p], 16 * ((t - p) // 2 + 1) if isinstance(t, int) else 8 * (t - p) + 16)
                wait(pe, centred, t)
                for k in range(KC):
                    last = nc.tensor.matmul(stat[0][:, :], mean_w[:, :], x[p][:, k, :],
                                            start=k == 0, stop=k == KC - 1)
                last.then_inc(mean_ready, 1)

            def var(t):
                pe.wait_ge(squared, t + 1)
                wait(pe, std_ready, t)
                for k in range(KC):
                    last = nc.tensor.matmul(stat[1][:, :], mean_w[:, :], sq[:, k, :],
                                            start=k == 0, stop=k == KC - 1)
                last.then_inc(var_ready, 1)

            def up(t, p, m):
                u = t * MC + m
                if m == 0:
                    pe.wait_ge(zlo_ready, t + 1)
                wait(pe, gelu_ready, u + 1 - NH)
                n = 0
                for a, b in PARTS:
                    for k in range(KC):
                        last = nc.tensor.matmul(hid[m % NH][:, :], wi[a][:, k, m * P:(m + 1) * P],
                                                z[p][b][:, k, :], start=n == 0, stop=n == 8)
                        n += 1
                last.then_inc(hid_ready, 1)

            def down(t, m):
                u = t * MC + m
                pe.wait_ge(ghi_ready, u + 1)
                pe.wait_ge(glo_ready, u + 1)
                for j in range(KC):
                    if m == 0:
                        wait(pe, evicted, KC * t - KC + j + 1)
                    for n, (a, b) in enumerate(PARTS):
                        last = nc.tensor.matmul(acc[j][:, :], wo[a][:, m, j * P:(j + 1) * P],
                                                gs[m % NS][b][:, :], start=m == 0 and n == 0,
                                                stop=m == MC - 1 and n == 2)
                last.then_inc(out_used, 1)

            def body(t, p, first, last):
                for m in range(MC):
                    up(t, p, m)
                    if m >= LAG:
                        down(t, m - LAG)
                    elif not first:
                        down(t - 1, MC + m - LAG)
                    if not last and m == 4:
                        mean(t + 1, 1 - p)
                    if not last and m == 6:
                        var(t + 1)
                if last:
                    for m in range(MC - LAG, MC):
                        down(t, m)

            pe.wait_ge(const_set, 1)
            mean(0, 0)
            var(0)
            pe.wait_ge(w_split, 4)
            tiles(nc.tensor, body)

        @block.vector
        def _(dve):
            nc.vector.memset(mean_w[:, :], 1.0 / C)
            nc.vector.memset(eps[:, :], EPS).then_inc(const_set, 1)

            def split_weights(loaded, hi, lo, step):
                dve.wait_ge(w_loaded, loaded)
                h, l = (v[:, :, :].rearrange("p k n -> p (k n)") for v in (hi, lo))
                nc.vector.tensor_scalar(h, stage_w[:, :], WSCALE, None, ALU.mult).then_inc(w_split, 1)
                dve.wait_ge(w_split, step + 1)
                nc.vector.scalar_tensor_tensor(l, stage_w[:, :], WSCALE, h, ALU.mult,
                                               ALU.subtract).then_inc(w_split, 1)

            def centre(t, p):
                dve.wait_ge(mean_ready, t + 1)
                wait(dve, zlo_ready, t)
                wait(dve, zhi_ready, t)
                nc.vector.tensor_tensor(d[:, :, :], x[p][:, :, :],
                                        stat[0][:, None, :].broadcast_to([P, KC, BANK]),
                                        ALU.subtract).then_inc(centred, 1)

            def invert(t):
                dve.wait_ge(std_ready, t + 1)
                nc.vector.reciprocal(std[:, :], std[:, :]).then_inc(inv_ready, 1)

            def normalise(t):
                dve.wait_ge(inv_ready, t + 1)
                dve.wait_ge(squared, t + 1)
                nc.vector.tensor_tensor(d[:, :, :], d[:, :, :],
                                        std[:, None, :].broadcast_to([P, KC, BANK]),
                                        ALU.mult).then_inc(z_ready, 1)

            def low(t, p):
                dve.wait_ge(z_ready, t + 1)
                dve.wait_ge(zhi_ready, t + 1)
                nc.vector.tensor_tensor(z[p][1][:, :, :], d[:, :, :], z[p][0][:, :, :],
                                        ALU.subtract).then_inc(zlo_ready, 1)

            def gelu_low(t, m):
                u = t * MC + m
                dve.wait_ge(ghi_ready, u + 1)
                wait(dve, out_used, u + 1 - NS)
                nc.vector.tensor_tensor(gs[m % NS][1][:, :], g[m % NG][:, :], gs[m % NS][0][:, :],
                                        ALU.subtract).then_inc(glo_ready, 1)

            def evict(t, p):
                dve.wait_ge(out_used, (t + 1) * MC)
                if isinstance(t, int):
                    wait(dve, stored[p], 16 * ((t - p) // 2))
                else:
                    dve.wait_ge(stored[p], 8 * (t - p))
                for j in range(KC):
                    nc.vector.scalar_tensor_tensor(ob[p][:, j, :], acc[j][:, :], 1.0 / WSCALE,
                                                   x[p][:, j, :], ALU.mult, ALU.add
                                                   ).then_inc(evicted, 1)

            def body(t, p, first, last):
                for m in range(MC):
                    gelu_low(t, m)
                    if m == 1 and not first:
                        evict(t - 1, 1 - p)
                    if not last:
                        if m == 5:
                            centre(t + 1, 1 - p)
                        if m == 8:
                            invert(t + 1)
                            normalise(t + 1)
                        if m == 10:
                            low(t + 1, 1 - p)
                if last:
                    evict(t, p)

            split_weights(32, wi[0], wi[1], 0)
            centre(0, 0)
            invert(0)
            normalise(0)
            low(0, 0)
            split_weights(48, wo[0], wo[1], 2)
            tiles(nc.vector, body)

        @block.scalar
        def _(act):
            def square(t):
                act.wait_ge(centred, t + 1)
                wait(act, var_ready, t)
                nc.scalar.activation(sq[:, :, :], d[:, :, :], ACT.Square).then_inc(squared, 1)

            def root(t):
                act.wait_ge(var_ready, t + 1)
                wait(act, z_ready, t)
                nc.scalar.activation(std[:, :], stat[1][:, :], ACT.Sqrt, bias=eps[:, 0:1]
                                     ).then_inc(std_ready, 1)

            def high(t, p):
                act.wait_ge(z_ready, t + 1)
                wait(act, hid_ready, (t - 1) * MC)
                nc.scalar.activation(z[p][0][:, :, :], d[:, :, :], ACT.Copy).then_inc(zhi_ready, 1)

            def gelu(t, m):
                u = t * MC + m
                act.wait_ge(hid_ready, u + 1)
                wait(act, glo_ready, u + 1 - NG)
                wait(act, out_used, u + 1 - NS)
                nc.scalar.activation(g[m % NG][:, :], hid[m % NH][:, :], ACT.Gelu,
                                     bias=bias[:, m:m + 1], scale=1.0 / WSCALE
                                     ).then_inc(gelu_ready, 1)
                act.wait_ge(gelu_ready, u + 1)
                nc.scalar.activation(gs[m % NS][0][:, :], g[m % NG][:, :], ACT.Copy
                                     ).then_inc(ghi_ready, 1)

            def body(t, p, first, last):
                for m in range(MC):
                    gelu(t, m)
                    if not last:
                        if m == 5:
                            square(t + 1)
                        if m == 7:
                            root(t + 1)
                        if m == 9:
                            high(t + 1, 1 - p)

            act.wait_ge(const_set, 1)
            square(0)
            root(0)
            high(0, 0)
            act.wait_ge(w_loaded, 32)
            tiles(nc.scalar, body)


def program(nc, x, conv_main, conv_corr, group_mean, masks, selectors, corr_start,
            w_q, w_k, w_v, w_o, b_o, identity, w_in, b_in, w_out, out):
    n_images = x.shape[0]
    after_conv = nc.dram_tensor("after_conv", [n_images, C, NPIX], F32, kind="Internal").ap()
    after_attention = nc.dram_tensor("after_attention", [n_images, C, NPIX], F32,
                                     kind="Internal").ap()
    conv_stage(nc, x, conv_main, conv_corr, group_mean, masks, selectors, corr_start,
               after_conv, n_images)
    attention_stage(nc, after_conv, w_q, w_k, w_v, w_o, b_o, identity, after_attention, n_images)
    ffn_stage(nc, after_attention, w_in, b_in, w_out, out, n_images)


def kernel(x, L0_conv_conv_w, L0_conv_conv_b, L1_attn_Wq, L1_attn_Wk, L1_attn_Wv, L1_attn_Wo,
           L1_attn_bo, L1_ffn_in_weight, L1_ffn_in_bias, L1_ffn_out_weight):
    import numpy as np
    import concourse.bacc as bacc
    from concourse.bass_utils import run_bass_kernel_spmd

    def per_partition(bias):
        return np.asarray(bias).reshape(-1, P).T

    x = np.asarray(x)
    conv_w = np.asarray(L0_conv_conv_w)
    corr = [conv_w[:, C + at] for at in corr_weight_rows()] + [np.asarray(L0_conv_conv_b)]
    constants = conv_constants()
    arrays = {
        "x": x.reshape(x.shape[0], C, NPIX),
        "conv_main": conv_w[:, :C].T,
        "conv_corr": np.stack(corr),
        **constants,
        "w_q": np.asarray(L1_attn_Wq).T,
        "w_k": np.asarray(L1_attn_Wk).T,
        "w_v": np.asarray(L1_attn_Wv).T,
        "w_o": np.asarray(L1_attn_Wo).T,
        "b_o": per_partition(L1_attn_bo),
        "identity": np.eye(P, dtype=np.float32),
        "w_in": np.asarray(L1_ffn_in_weight).T,
        "b_in": per_partition(L1_ffn_in_bias),
        "w_out": np.asarray(L1_ffn_out_weight),
    }
    arrays = {f"in_{name}": np.ascontiguousarray(a) for name, a in arrays.items()}
    nc = bacc.Bacc("TRN2", target_bir_lowering=False, num_devices=1)
    args = [nc.dram_tensor(name, a.shape, mybir.dt.from_np(a.dtype), kind="ExternalInput").ap()
            for name, a in arrays.items()]
    out = nc.dram_tensor("out", [x.shape[0], C, NPIX], F32, kind="ExternalOutput").ap()
    program(nc, *args, out)
    result = run_bass_kernel_spmd(nc, [arrays], core_ids=[0])
    return result.results[0]["out"].reshape(x.shape)
```

```python
from contextlib import ExitStack

import concourse.bass as bass
from concourse import mybir

F32 = mybir.dt.float32
F16 = mybir.dt.float16
ALU = mybir.AluOpType
ACT = mybir.ActivationFunctionType
AX_X = mybir.AxisListType.X

C = 384
NPIX = 1024
P = 128
KC = C // P
ROW = 32
BANK = 512
HALVES = NPIX // BANK
WSCALE = 256.0
PARTS = [(0, 0), (0, 1), (1, 0)]


def wait(eng, sem, value):
    if isinstance(value, int) and value <= 0:
        return
    eng.wait_ge(sem, value)


def wait_both(eng, first, second):
    ready = [(s, v if isinstance(v, int) else eng.to_reg(v)) for s, v in (first, second)]
    for s, v in ready:
        wait(eng, s, v)


class Names:

    def __init__(self, nc, ctx, prefix):
        self.nc, self.ctx, self.prefix = nc, ctx, prefix

    def sb(self, name, shape, dt=F32):
        return self.ctx.enter_context(self.nc.sbuf_tensor(f"{self.prefix}_{name}", shape, dt))

    def ps(self, name, shape, dt=F32):
        return self.ctx.enter_context(self.nc.psum_tensor(f"{self.prefix}_{name}", shape, dt))

    def sem(self, name):
        return self.ctx.enter_context(self.nc.semaphore(f"{self.prefix}_{name}"))


def image_tile(dram, image, lo=0, n=NPIX):
    return dram[bass.ds(image, 1), :, lo:lo + n].rearrange("a (k p) n -> p (a k) n", p=P)


K7 = 7
PAD = K7 // 2
REFERENCE_SHIFTS = ([(i - PAD, i - PAD) for i in range(K7)] + [(i - PAD, 0) for i in range(K7)]
                    + [(i - PAD, PAD - i) for i in range(K7)] + [(0, i - PAD) for i in range(K7)])
KINDS = 3


def forward_column(kind, dr):
    return kind + 1 if dr == 0 else (kind - 1) * dr


FORWARD = [(dr, forward_column(kind, dr)) for dr in range(PAD + 1) for kind in range(KINDS)]
NF = len(FORWARD)
SELF = REFERENCE_SHIFTS.count((0, 0))
CORR_ROWS = FORWARD + [(0, 0)] * SELF + [(-r, -c) for r, c in FORWARD]
NC = len(CORR_ROWS)
BACK = NF + SELF
CB = 32


def conv_stage(nc, x_in, w_main, w_corr, group_mean, masks, selectors, corr_start, out, n_images):
    EPS = 1e-5
    NORM_EPS = 1e-12
    WINDOW = (PAD + 1) * ROW
    PADDED = NPIX + PAD * ROW
    EV = KC * HALVES
    SETUP = 9
    CONSTANTS = 16 * 5
    ctx = ExitStack()
    with ctx:
        N = Names(nc, ctx, "a")
        stage_w = N.sb("stage_w", [P, KC * C])
        stage_c = N.sb("stage_c", [NC + 1, C])
        wm = [N.sb(f"wm{s}", [P, KC, C], F16) for s in range(2)]
        wc = N.sb("wc", [3 * CB, C], F16)
        gmean = N.sb("gmean", [P, KC * KC, P])
        mask = N.sb("mask", [P, KINDS + 1, ROW])
        sel = N.sb("sel", [P, KINDS + 1, BACK])
        ones = N.sb("ones", [P, P])
        eps = N.sb("eps", [P, 1])
        x = [N.sb(f"x{p}", [P, KC, NPIX]) for p in range(2)]
        bn = N.sb("bn", [P, KC, HALVES, 6])
        mv = N.sb("mv", [P, KC, 2])
        gm = N.sb("gm", [P, KC])
        dm = N.sb("dm", [P, KC])
        ev = N.sb("ev", [P, KC])
        rs = N.sb("rs", [P, KC])
        f = [N.sb(f"f{p}", [P, KC, NPIX]) for p in range(2)]
        sq = N.sb("sq", [P, KC, NPIX])
        sqs = N.sb("sqs", [P, NPIX])
        fs = [[N.sb(f"fs{p}{s}", [P, KC, NPIX], F16) for s in range(2)] for p in range(2)]
        nrm = N.sb("nrm", [P, NPIX])
        fn = [N.sb(f"fn{s}", [P, KC, PADDED], F16) for s in range(2)]
        picked = N.sb("picked", [P, KINDS + 1, NPIX])
        cs = [N.sb(f"cs{p}", [3 * CB, NPIX], F16) for p in range(2)]
        ob = [N.sb(f"ob{p}", [P, KC, NPIX]) for p in range(2)]
        stat = N.ps("stat", [P, NPIX])
        gram = N.ps("gram", [P, NPIX])
        corr = N.ps("corr", [P, NPIX])
        conv = [N.ps(f"conv{k}", [P, BANK]) for k in range(2)]

        w_loaded = N.sem("w_loaded")
        c_loaded = N.sem("c_loaded")
        set_up = N.sem("set_up")
        x_loaded = [N.sem(f"x_loaded{p}") for p in range(2)]
        moved = [N.sem(f"moved{p}") for p in range(2)]
        shifted = [N.sem(f"shifted{p}") for p in range(2)]
        stored = [N.sem(f"stored{p}") for p in range(2)]
        mv_ready = N.sem("mv_ready")
        gmean_ready = N.sem("gmean_ready")
        spread = N.sem("spread")
        gvar_ready = N.sem("gvar_ready")
        gstd_ready = N.sem("gstd_ready")
        ginv_ready = N.sem("ginv_ready")
        f_ready = N.sem("f_ready")
        squared = N.sem("squared")
        folded = N.sem("folded")
        ssq_ready = N.sem("ssq_ready")
        norm_ready = N.sem("norm_ready")
        clamped = N.sem("clamped")
        fn_ready = N.sem("fn_ready")
        fnhi_ready = N.sem("fnhi_ready")
        fnlo_ready = N.sem("fnlo_ready")
        fhi_ready = N.sem("fhi_ready")
        flo_ready = N.sem("flo_ready")
        gram_ready = N.sem("gram_ready")
        masked = N.sem("masked")
        corr_ready = N.sem("corr_ready")
        chi_ready = N.sem("chi_ready")
        clo_ready = N.sem("clo_ready")
        conv_ready = N.sem("conv_ready")
        evicted = N.sem("evicted")
        block = ctx.enter_context(nc.Block())

        def real(i):
            return not isinstance(i, int) or 0 <= i < n_images

        def half(h):
            return slice(h * BANK, (h + 1) * BANK)

        def steps(eng, step):
            for s in range(-2, 2):
                step(s, s % 2)
            with eng.Fori(1, n_images // 2 - 1) as pair:
                step(2 * pair, 0)
                step(2 * pair + 1, 1)
            for s in range(n_images - 2, n_images + 1):
                step(s, s % 2)

        def dmas(i, p, n=1):
            return 16 * n * ((i - p) // 2 + 1) if isinstance(i, int) else 8 * n * (i - p + 2)

        @block.sync
        def _(sp):
            def load(i, p):
                sp.dma_start(x[p][:, :, :], image_tile(x_in, i)).then_inc(x_loaded[p], 16)

            load(0, 0)
            for dst, src in ((gmean[:, :, :], group_mean), (mask[:, :, :], masks),
                             (sel[:, :, :], selectors), (cs[0][:, :], corr_start),
                             (cs[1][:, :], corr_start)):
                sp.dma_start(dst, src).then_inc(c_loaded, 16)
            load(1, 1)
            sp.dma_start(stage_w[:, :].rearrange("p (k n) -> p k n", k=KC),
                         w_main.rearrange("(k p) n -> p k n", p=P)).then_inc(w_loaded, 16)
            sp.dma_start(stage_c[:, :], w_corr).then_inc(w_loaded, 16)

            def step(s, p):
                q = 1 - p
                if real(s) and real(s + 2):
                    wait_both(sp, (moved[p], dmas(s, p)), (f_ready, KC * (s + 1)))
                    load(s + 2, p)
                if real(s - 1):
                    wait_both(sp, (chi_ready, 2 * s), (clo_ready, s))
                    for n, (dr, dc) in enumerate(FORWARD):
                        d = dr * ROW + dc
                        sp.dma_start(cs[q][BACK + n:BACK + n + 2 * CB + 1:CB, d:NPIX],
                                     cs[q][n:n + 2 * CB + 1:CB, 0:NPIX - d]).then_inc(shifted[q], 16)
                for j in range(KC if real(s - 1) else 0):
                    sp.wait_ge(evicted, EV * (s - 1) + HALVES * (j + 1))
                    sp.dma_start(image_tile(out, s - 1)[:, j:j + 1, :], ob[q][:, j:j + 1, :]
                                 ).then_inc(stored[q], 16)
                if real(s + 1):
                    if real(s - 1):
                        wait_both(sp, (stored[q], dmas(s - 1, q, KC)), (x_loaded[q], dmas(s + 1, q)))
                    else:
                        sp.wait_ge(x_loaded[q], dmas(s + 1, q))
                    sp.dma_start(ob[q][:, :, :], x[q][:, :, :]).then_inc(moved[q], 16)

            steps(sp, step)
            for p in range(2):
                sp.wait_ge(stored[p], dmas(n_images - 2 + p, p, KC))

        @block.tensor
        def _(pe):
            def average(dst, column, source, done):
                for j in range(KC):
                    near = [k for k in range(KC) if abs(j - k) <= 1]
                    for k in near:
                        last = nc.tensor.matmul(dst[:, column + j:column + j + 1], gmean[:, k * KC + j, :],
                                                source(k), start=k == near[0], stop=k == near[-1])
                last.then_inc(done, 1)

            def correlate(h):
                for r in range(h * BANK // ROW, (h + 1) * BANK // ROW):
                    n = 0
                    for a, b in PARTS:
                        for k in range(KC):
                            last = nc.tensor.matmul(
                                gram[:, r * ROW:(r + 1) * ROW],
                                fn[a][:, k, r * ROW:r * ROW + WINDOW],
                                fn[b][:, k, r * ROW:(r + 1) * ROW], start=n == 0, stop=n == 8)
                            n += 1
                last.then_inc(gram_ready, 1)

            def select(i, h):
                pe.wait_ge(masked, 2 * i + 1 + h)
                for kind in range(KINDS + 1):
                    last = nc.tensor.matmul(corr[0:BACK, half(h)], sel[:, kind, :],
                                            picked[:, kind, half(h)],
                                            start=kind == 0, stop=kind == KINDS)
                last.then_inc(corr_ready, 1)

            def squared_norms(i):
                pe.wait_ge(folded, 2 * i + 2)
                pe.wait_ge(gstd_ready, i + 1)
                pe.wait_ge(spread, 3 * i + 1)
                for h in range(HALVES):
                    nc.tensor.matmul(stat[:, half(h)], ones[:, :], sqs[:, half(h)],
                                     start=True, stop=True).then_inc(ssq_ready, 1)

            def convolve(i, p):
                if isinstance(i, int) and i == 0:
                    pe.wait_ge(set_up, SETUP)
                pe.wait_ge(fhi_ready, KC * (i + 1))
                pe.wait_ge(flo_ready, KC * (i + 1))
                pe.wait_ge(shifted[p], dmas(i, p, NF))
                for n in range(EV):
                    j, h = n // HALVES, n % HALVES
                    wait(pe, evicted, EV * i + n - 1)
                    nc.tensor.matmul(conv[n % 2][:, :], wc[:, j * P:(j + 1) * P], cs[p][:, half(h)],
                                     start=True, stop=False)
                    m = 0
                    for a, b in PARTS:
                        for k in range(KC):
                            last = nc.tensor.matmul(conv[n % 2][:, :], wm[a][:, k, j * P:(j + 1) * P],
                                                    fs[p][b][:, k, half(h)], start=False, stop=m == 8)
                            m += 1
                    last.then_inc(conv_ready, 1)

            def step(s, p):
                if real(s):
                    pe.wait_ge(fnlo_ready, KC * (s + 1))
                    pe.wait_ge(fnhi_ready, KC * (s + 1))
                    wait(pe, masked, 2 * s)
                    correlate(0)
                if real(s + 1):
                    squared_norms(s + 1)
                if real(s):
                    correlate(1)
                if real(s + 2):
                    pe.wait_ge(mv_ready, s + 3)
                    wait(pe, norm_ready, 2 * (s + 2))
                    average(stat, 0, lambda k: mv[:, k, 0:1], gmean_ready)
                if real(s - 1):
                    convolve(s - 1, 1 - p)
                if real(s + 2):
                    pe.wait_ge(spread, 3 * (s + 2) + 3)
                    average(stat, BANK, lambda k: ev[:, k:k + 1], gvar_ready)
                if real(s):
                    wait(pe, chi_ready, 2 * s)
                    wait(pe, clo_ready, s)
                    select(s, 0)
                    select(s, 1)

            pe.wait_ge(c_loaded, CONSTANTS)
            pe.wait_ge(set_up, 3)
            steps(nc.tensor, step)

        @block.vector
        def _(dve):
            nc.vector.memset(ones[:, :], 1.0).then_inc(set_up, 1)
            nc.vector.memset(wc[:, :], 0.0).then_inc(set_up, 1)
            for t in fn:
                last = nc.vector.memset(t[:, :, NPIX:PADDED], 0.0)
            last.then_inc(set_up, 1)
            nc.vector.memset(eps[:, :], EPS).then_inc(set_up, 1)

            def weights():
                dve.wait_ge(w_loaded, 32)
                dve.wait_ge(set_up, 4)
                h, l = (v[:, :, :].rearrange("p k n -> p (k n)") for v in wm)
                nc.vector.tensor_scalar(h, stage_w[:, :], WSCALE, None, ALU.mult).then_inc(set_up, 1)
                nc.vector.tensor_scalar(wc[0:NC + 1, :], stage_c[:, :], WSCALE, None, ALU.mult
                                        ).then_inc(set_up, 1)
                dve.wait_ge(set_up, 6)
                nc.vector.scalar_tensor_tensor(l, stage_w[:, :], WSCALE, h, ALU.mult,
                                               ALU.subtract).then_inc(set_up, 1)
                nc.vector.tensor_copy(wc[CB:CB + NC + 1, :], wc[0:NC + 1, :]).then_inc(set_up, 1)
                nc.vector.scalar_tensor_tensor(wc[2 * CB:2 * CB + NC + 1, :], stage_c[:, :], WSCALE,
                                               wc[0:NC + 1, :], ALU.mult, ALU.subtract
                                               ).then_inc(set_up, 1)

            def keep_shifts(i, h):
                dve.wait_ge(gram_ready, 2 * i + 1 + h)
                for kind in range(KINDS + 1):
                    last = nc.vector.tensor_tensor(
                        picked[:, kind, half(h)].rearrange("p (r c) -> p r c", c=ROW),
                        gram[:, half(h)].rearrange("p (r c) -> p r c", c=ROW),
                        mask[:, kind, None, :].broadcast_to([P, BANK // ROW, ROW]), ALU.mult)
                last.then_inc(masked, 1)

            def invert_norms(i, h):
                dve.wait_ge(norm_ready, 2 * i + 1 + h)
                nc.vector.tensor_scalar(nrm[:, half(h)], nrm[:, half(h)], NORM_EPS, None, ALU.max
                                        ).then_inc(clamped, 1)
                dve.wait_ge(clamped, 4 * i + 2 * h + 1)
                nc.vector.reciprocal(nrm[:, half(h)], nrm[:, half(h)]).then_inc(clamped, 1)

            def unit_features(i, p, n):
                if n < KC:
                    dve.wait_ge(clamped, 4 * i + 4)
                    nc.vector.tensor_tensor(sq[:, n, :], f[p][:, n, :], nrm[:, :], ALU.mult
                                            ).then_inc(fn_ready, 1)
                else:
                    k = n - KC
                    dve.wait_ge(fn_ready, KC * i + k + 1)
                    dve.wait_ge(fnhi_ready, KC * i + k + 1)
                    nc.vector.tensor_tensor(fn[1][:, k, 0:NPIX], sq[:, k, :], fn[0][:, k, 0:NPIX],
                                            ALU.subtract).then_inc(fnlo_ready, 1)

            def evict(i, p, n):
                j, h = n // HALVES, n % HALVES
                if n == 0:
                    dve.wait_ge(moved[p], dmas(i, p))
                dve.wait_ge(conv_ready, EV * i + n + 1)
                nc.vector.scalar_tensor_tensor(ob[p][:, j, half(h)], conv[n % 2][:, :], 1.0 / WSCALE,
                                               ob[p][:, j, half(h)], ALU.mult, ALU.add
                                               ).then_inc(evicted, 1)

            def statistics(i, p):
                dve.wait_ge(x_loaded[p], dmas(i, p))
                for k in range(KC):
                    for h in range(HALVES):
                        nc.vector.bn_stats(bn[:, k, h, :], x[p][:, k, half(h)])
                dve.drain()
                for k in range(KC):
                    last = nc.vector.bn_aggr(mv[:, k, :], bn[:, k, :, :])
                last.then_inc(mv_ready, 1)

            def within_groups(i):
                dve.wait_ge(gmean_ready, i + 1)
                dve.wait_ge(mv_ready, i + 1)
                nc.vector.tensor_copy(gm[:, :], stat[:, 0:KC])
                nc.vector.tensor_tensor(dm[:, :], mv[:, :, 0], stat[:, 0:KC], ALU.subtract
                                        ).then_inc(spread, 1)
                dve.wait_ge(spread, 3 * i + 1)
                nc.vector.tensor_tensor(ev[:, :], dm[:, :], dm[:, :], ALU.mult).then_inc(spread, 1)
                dve.wait_ge(spread, 3 * i + 2)
                nc.vector.tensor_tensor(ev[:, :], ev[:, :], mv[:, :, 1], ALU.add).then_inc(spread, 1)

            def features(i, p):
                dve.wait_ge(gstd_ready, i + 1)
                nc.vector.reciprocal(rs[:, :], rs[:, :]).then_inc(ginv_ready, 1)
                dve.wait_ge(ginv_ready, i + 1)
                wait(dve, flo_ready, KC * (i - 1))
                for k in range(KC):
                    nc.vector.tensor_scalar(f[p][:, k, :], x[p][:, k, :], gm[:, k:k + 1],
                                            rs[:, k:k + 1], ALU.subtract, ALU.mult
                                            ).then_inc(f_ready, 1)

            def step(s, p):
                if real(s):
                    wait(dve, corr_ready, 2 * s)
                    keep_shifts(s, 0)
                if real(s + 2):
                    statistics(s + 2, p)
                if real(s + 1):
                    invert_norms(s + 1, 0)
                    invert_norms(s + 1, 1)
                if real(s):
                    keep_shifts(s, 1)
                if real(s + 2):
                    within_groups(s + 2)
                if isinstance(s, int) and s == -1:
                    weights()
                for n in range(EV):
                    if real(s - 1):
                        evict(s - 1, 1 - p, n)
                    if real(s + 1):
                        unit_features(s + 1, 1 - p, n)
                if real(s + 2):
                    features(s + 2, p)
                if real(s):
                    dve.wait_ge(chi_ready, 2 * s + 1)
                    nc.vector.tensor_tensor(cs[p][CB:CB + BACK, :], corr[0:BACK, :], cs[p][0:BACK, :],
                                            ALU.subtract).then_inc(clo_ready, 1)

            dve.wait_ge(c_loaded, CONSTANTS)
            steps(nc.vector, step)

        @block.scalar
        def _(act):
            def step(s, p):
                q = 1 - p
                if real(s + 1):
                    wait(act, fn_ready, KC * (s + 1))
                    for h in range(HALVES):
                        act.wait_ge(ssq_ready, 2 * (s + 1) + 1 + h)
                        nc.scalar.activation(nrm[:, half(h)], stat[:, half(h)], ACT.Sqrt
                                             ).then_inc(norm_ready, 1)
                    wait(act, gram_ready, 2 * (s + 1))
                    for k in range(KC):
                        act.wait_ge(fn_ready, KC * (s + 1) + k + 1)
                        nc.scalar.activation(fn[0][:, k, 0:NPIX], sq[:, k, :], ACT.Copy
                                             ).then_inc(fnhi_ready, 1)
                if real(s + 2):
                    act.wait_ge(gvar_ready, s + 3)
                    wait(act, f_ready, KC * (s + 2))
                    nc.scalar.activation(rs[:, :], stat[:, BANK:BANK + KC], ACT.Sqrt, bias=eps[:, 0:1]
                                         ).then_inc(gstd_ready, 1)
                if real(s + 1):
                    wait(act, conv_ready, EV * s)
                    for k in range(KC):
                        nc.scalar.activation(fs[q][0][:, k, :], f[q][:, k, :], ACT.Copy
                                             ).then_inc(fhi_ready, 1)
                if real(s + 2):
                    for k in range(KC):
                        act.wait_ge(f_ready, KC * (s + 2) + k + 1)
                        if real(s + 1):
                            act.wait_ge(fnlo_ready, KC * (s + 1) + k + 1)
                        nc.scalar.activation(sq[:, k, :], f[p][:, k, :], ACT.Square
                                             ).then_inc(squared, 1)
                if real(s):
                    act.wait_ge(corr_ready, 2 * s + 2)
                    wait(act, conv_ready, EV * (s - 1))
                    nc.scalar.activation(cs[p][0:BACK, :], corr[0:BACK, :], ACT.Copy
                                         ).then_inc(chi_ready, 1)
                    act.wait_ge(chi_ready, 2 * s + 1)
                    nc.scalar.activation(cs[p][2 * CB:2 * CB + BACK, :], cs[p][0:BACK, :], ACT.Copy
                                         ).then_inc(chi_ready, 1)

            act.wait_ge(set_up, 4)
            act.wait_ge(c_loaded, CONSTANTS)
            steps(nc.scalar, step)

        @block.gpsimd
        def _(pool):
            def step(s, p):
                q = 1 - p
                if real(s + 2):
                    pool.wait_ge(squared, KC * (s + 2) + 2)
                    wait(pool, ssq_ready, 2 * (s + 2))
                    nc.gpsimd.tensor_tensor(sqs[:, :], sq[:, 0, :], sq[:, 1, :], ALU.add
                                            ).then_inc(folded, 1)
                    pool.wait_ge(folded, 2 * (s + 2) + 1)
                    pool.wait_ge(squared, KC * (s + 3))
                    nc.gpsimd.tensor_tensor(sqs[:, :], sqs[:, :], sq[:, 2, :], ALU.add
                                            ).then_inc(folded, 1)
                if real(s + 1):
                    for k in range(KC):
                        pool.wait_ge(fhi_ready, KC * (s + 1) + k + 1)
                        nc.gpsimd.tensor_tensor(fs[q][1][:, k, :], f[q][:, k, :], fs[q][0][:, k, :],
                                                ALU.subtract).then_inc(flo_ready, 1)

            steps(nc.gpsimd, step)


def conv_constants():
    import numpy as np

    group = C // 32
    of = np.arange(C) // group
    mean = (of[:, None] == of[None, :]).astype(np.float32) / np.float32(group)
    mean = mean.reshape(KC, P, KC, P).transpose(1, 0, 2, 3).reshape(P, KC * KC, P)
    masks = np.zeros((P, KINDS + 1, ROW), np.float32)
    sel = np.zeros((P, KINDS + 1, BACK), np.float32)
    for dr in range(PAD + 1):
        for q in range(ROW):
            for kind in range(KINDS):
                col = q - forward_column(kind, dr)
                if 0 <= col < ROW:
                    masks[dr * ROW + q, kind, col] = 1
                sel[dr * ROW + q, kind, FORWARD.index((dr, forward_column(kind, dr)))] = 1
            if dr == 0:
                masks[q, KINDS, q] = 1
                sel[q, KINDS, NF:BACK] = 1
    start = np.zeros((3 * CB, NPIX), np.float16)
    start[NC] = 1
    start[2 * CB + NC] = 1
    return {"group_mean": np.ascontiguousarray(mean), "masks": masks, "selectors": sel, "corr_start": start}


def corr_weight_rows():
    left = list(enumerate(REFERENCE_SHIFTS))
    rows = []
    for shift in CORR_ROWS:
        at = next(n for n, (_, s) in enumerate(left) if s == shift)
        rows.append(left.pop(at)[0])
    return rows


def attention_stage(nc, x_in, w_q, w_k, w_v, w_o, b_o, identity, out, n_images):
    HEAD = 32
    HG = P // HEAD
    GROUPS = KC
    STEPS = HG
    SCORES = 2 * STEPS
    NST = 3
    UNITS = 8
    IU = UNITS * GROUPS
    TILES = NPIX // P
    ITEMS = HG * TILES * HALVES
    MAXROW = 3 * HEAD
    SCALE = HEAD ** -0.5
    EPS = 1e-5
    QUARTER = BANK // 4
    NQKV = 6 * GROUPS
    FIRST = 6
    STACKED = 16 * (6 * HG + 1)
    ctx = ExitStack()
    with ctx:
        N = Names(nc, ctx, "b")
        ws = [[N.sb(f"w{n}{s}", [P, KC, C], F16) for s in range(2)] for n in "qkvo"]
        bo = N.sb("bo", [P, KC])
        ident = N.sb("ident", [P, P])
        mean_w = N.sb("mean_w", [P, P])
        ones = N.sb("ones", [P, HEAD])
        eps = N.sb("eps", [P, 1])
        xl = N.sb("xl", [P, KC, NPIX])
        xs = [N.sb(f"xs{h}", [P, BANK]) for h in range(HALVES)]
        std = xs
        z = [N.sb(f"z{s}", [P, KC, NPIX], F16) for s in range(2)]
        sq = z[1][:, :, :].rearrange("p k n -> p (k n)").bitcast(F32).rearrange(
            "p (k n) -> p k n", k=KC)
        staged = [[[N.sb(f"staged{e}{n}{s}", [P, NPIX], F16) for s in range(2)] for n in "qk"]
                  for e in range(2)]
        vstaged = N.sb("vstaged", [P, TILES, P])
        qst = [N.sb(f"qst{g}", [P, HG, NPIX], F16) for g in range(GROUPS)]
        kst = [N.sb(f"kst{g}", [P, HG, NPIX], F16) for g in range(GROUPS)]
        v = [N.sb(f"v{g}", [P, TILES, P]) for g in range(GROUPS)]
        mxp = [N.sb(f"mxp{e}", [P, TILES, HALVES]) for e in range(2)]
        nm = [N.sb(f"nm{e}", [P, TILES]) for e in range(2)]
        mr = [N.sb(f"mr{e}", [TILES, P], F16) for e in range(2)]
        ex = [N.sb(f"ex{k}", [P, NPIX]) for k in range(2 * HG)]
        pair = [N.sb(f"pair{k}", [P, BANK]) for k in range(2 * HG)]
        pvs = N.sb("pvs", [P, BANK])
        inv = N.sb("inv", [P, BANK])
        ao = [N.sb(f"ao{s}", [P, KC, NPIX], F16) for s in range(2)]
        ot = N.sb("ot", [P, BANK])
        xr = N.sb("xr", [P, KC, NPIX])
        room = [t[:, :, :].rearrange("p k n -> p (k n)") for t in (xr, ao[0], ao[1])]
        room = [room[0]] + [t.bitcast(F32) for t in room[1:]]
        stage_w = [room[0][:, 0:KC * C], room[0][:, KC * C:2 * KC * C], room[1][:, 0:KC * C],
                   room[2][:, 0:KC * C]]
        st = [N.ps(f"st{e}", [P, BANK]) for e in range(NST)]
        mx = [N.ps(f"mx{e}", [P, BANK]) for e in range(2)]
        pj = N.ps("pj", [P, BANK])
        pv = N.ps("pv", [P, BANK])
        sm = N.ps("sm", [P, BANK])

        w_loaded = [N.sem(f"w_loaded{n}") for n in "qkvo"]
        w_high = N.sem("w_high")
        w_low = N.sem("w_low")
        c_loaded = N.sem("c_loaded")
        const_set = N.sem("const_set")
        row_of_ones = N.sem("row_of_ones")
        x_loaded = N.sem("x_loaded")
        x_folded = N.sem("x_folded")
        sq_folded = N.sem("sq_folded")
        mean_ready = N.sem("mean_ready")
        centred = N.sem("centred")
        squared = N.sem("squared")
        var_ready = N.sem("var_ready")
        std_ready = N.sem("std_ready")
        inv_ready = N.sem("inv_ready")
        z_ready = N.sem("z_ready")
        zhi_ready = N.sem("zhi_ready")
        zlo_ready = N.sem("zlo_ready")
        proj_ready = N.sem("proj_ready")
        hi_staged = N.sem("hi_staged")
        lo_staged = N.sem("lo_staged")
        v_staged = N.sem("v_staged")
        stacked = [N.sem(f"stacked{g}") for g in range(GROUPS)]
        mx_ready = N.sem("mx_ready")
        mx_taken = N.sem("mx_taken")
        combined = N.sem("combined")
        turned = N.sem("turned")
        row_ready = N.sem("row_ready")
        row_loaded = [N.sem(f"row_loaded{h}") for h in range(HG)]
        st_ready = N.sem("st_ready")
        exp_ready = N.sem("exp_ready")
        pair_ready = N.sem("pair_ready")
        pair_added = N.sem("pair_added")
        pv_ready = N.sem("pv_ready")
        sum_ready = N.sem("sum_ready")
        pv_moved = N.sem("pv_moved")
        sum_inverted = N.sem("sum_inverted")
        att_ready = N.sem("att_ready")
        ahi_ready = N.sem("ahi_ready")
        alo_ready = N.sem("alo_ready")
        o_ready = N.sem("o_ready")
        o_moved = N.sem("o_moved")
        o_added = N.sem("o_added")
        r_loaded = N.sem("r_loaded")
        stored = N.sem("stored")
        block = ctx.enter_context(nc.Block())

        def schedule(eng, prologue, unit, epilogue):
            last = n_images - 1
            prologue()
            for u in range(FIRST):
                unit(0, u, out_proj=False, norm=True)
            with eng.Fori(0, last - 1) as b:
                for u in range(FIRST, IU):
                    unit(b, u, load=True)
                for u in range(FIRST):
                    unit(b + 1, u)
            for u in range(FIRST, IU):
                unit(last - 1, u)
            for u in range(FIRST):
                unit(last, u, norm=False)
            for u in range(FIRST, IU):
                unit(last, u, norm=False, qkv=False, maxima=u < IU - UNITS)
            epilogue(last)

        def in_prologue(m):
            return isinstance(m, int) and m == 0

        def bank_of(m, i):
            return sm if in_prologue(m) and i % 2 else pj

        def prologue_items(i):
            first, each = 14, 6
            if i < first:
                return range(0)
            return range((i - first) * each, (i - first + 1) * each if i < NQKV - 1 else ITEMS)

        def turn_of(b, u):
            return HG * (GROUPS * b + u // UNITS + 1) + (u % UNITS) // 2 - 1

        @block.sync
        def _(sp):
            def load_x(m):
                wait(sp, zlo_ready, 2 * m)
                sp.dma_start(xl[:, :, :], image_tile(x_in, m)).then_inc(x_loaded, 16)

            def load_r(b):
                wait(sp, stored, 16 * b)
                sp.dma_start(xr[:, :, :], image_tile(x_in, b)).then_inc(r_loaded, 16)

            def stack(m, g):
                e = g % 2
                if in_prologue(m):
                    sp.wait_ge(lo_staged, 4 * g + 4)
                else:
                    wait_both(sp, (lo_staged, 12 * m + 4 * g + 4), (v_staged, 6 * m + 2 * g + 2))
                wait(sp, pv_ready, 2 * (IU * (m - 1) + UNITS * (g + 1)))
                for dst, part, (a, b, c) in ((qst, 0, (0, 1, 0)), (kst, 1, (0, 0, 1))):
                    for r, s in enumerate((a, b, c)):
                        for h in range(HG):
                            sp.dma_start(dst[g][r * HEAD:(r + 1) * HEAD, h, :],
                                         staged[e][part][s][h * HEAD:(h + 1) * HEAD, :]
                                         ).then_inc(stacked[g], 16)
                if in_prologue(m):
                    sp.wait_ge(v_staged, 2 * g + 2)
                sp.dma_start(v[g][:, :, :], vstaged[:, :, :]).then_inc(stacked[g], 16)

            def load_row(turn, g, h):
                sp.wait_ge(row_ready, turn + 1)
                sp.dma_start(qst[g][MAXROW:MAXROW + 1, h, :], mr[h % 2][:, :]).then_inc(row_loaded[h], 16)

            def prologue():
                load_x(0)
                for n, w in enumerate((w_q, w_k, w_v, w_o)):
                    sp.dma_start(stage_w[n].rearrange("p (k n) -> p k n", k=KC),
                                 w.rearrange("(k p) n -> p k n", p=P)).then_inc(w_loaded[n], 16)
                sp.dma_start(ident[:, :], identity).then_inc(c_loaded, 16)
                sp.dma_start(bo[:, :], b_o).then_inc(c_loaded, 16)
                stack(0, 0)
                stack(0, 1)
                sp.wait_ge(w_low, 4)
                load_r(0)
                load_x(1)
                stack(0, 2)
                for h in range(HG - 1):
                    load_row(h, 0, h)

            def unit(b, u, qkv=True, maxima=True):
                g, w = u // UNITS, u % UNITS
                if w == 0:
                    load_row(turn_of(b, u), g, HG - 1)
                elif w % 2 == 0 and maxima:
                    load_row(turn_of(b, u), (g + 1) % GROUPS, w // 2 - 1)
                if u == 0 and not (isinstance(b, int) and b == 0):
                    stack(b, 2)
                if u == 12 and qkv:
                    stack(b + 1, 0)
                if u == 18 and qkv:
                    stack(b + 1, 1)

            def epilogue(b):
                sp.wait_ge(o_added, 6 * (b + 1))
                sp.dma_start(image_tile(out, b), xr[:, :, :]).then_inc(stored, 16)
                sp.wait_ge(stored, 16 * (b + 1))

            last = n_images - 1
            prologue()
            for u in range(FIRST):
                unit(0, u)
            with sp.Fori(0, last - 1) as b:
                for u in range(FIRST, IU):
                    unit(b, u)
                    if u == FIRST:
                        load_x(b + 2)
                for u in range(FIRST):
                    unit(b + 1, u)
                sp.wait_ge(o_added, 6 * b + 6)
                sp.dma_start(image_tile(out, b), xr[:, :, :]).then_inc(stored, 16)
                load_r(b + 1)
            for u in range(FIRST, IU):
                unit(last - 1, u)
            for u in range(FIRST):
                unit(last, u)
            sp.wait_ge(o_added, 6 * last)
            sp.dma_start(image_tile(out, last - 1), xr[:, :, :]).then_inc(stored, 16)
            load_r(last)
            for u in range(FIRST, IU):
                unit(last, u, qkv=False, maxima=u < IU - UNITS)
            epilogue(last)

        @block.tensor
        def _(pe):
            free = {id(pj): None, id(sm): None}

            def take(bank, done, count):
                if free[id(bank)]:
                    wait(pe, *free[id(bank)])
                free[id(bank)] = (done, count)

            def mean(m, h):
                take(bank_of(m, h), centred, KC * (2 * m + h + 1))
                pe.wait_ge(x_folded, 4 * m + 2 * h + 2)
                nc.tensor.matmul(bank_of(m, h)[:, :], mean_w[:, :], xs[h][:, :], start=True, stop=True
                                 ).then_inc(mean_ready, 1)

            def var(m, h):
                take(bank_of(m, h), std_ready, 2 * m + h + 1)
                pe.wait_ge(sq_folded, 4 * m + 2 * h + 2)
                nc.tensor.matmul(bank_of(m, h)[:, :], mean_w[:, :], xs[h][:, :], start=True, stop=True
                                 ).then_inc(var_ready, 1)

            def project(m, i):
                g, kind, part = i // 6, (i % 6) // 2, i % 2
                if in_prologue(m) and i % 2 == 0 and g == 0:
                    pe.wait_ge(w_low, kind + 1)
                if kind < 2:
                    take(bank_of(m, i), lo_staged, 12 * m + 4 * g + 2 * kind + part + 1)
                    pe.wait_ge(zhi_ready, 2 * m + part + 1)
                    pe.wait_ge(zlo_ready, 2 * m + part + 1)
                else:
                    take(bank_of(m, i), v_staged, 6 * m + 2 * g + part + 1)
                    pe.wait_ge(zhi_ready, 2 * m + 2)
                    pe.wait_ge(zlo_ready, 2 * m + 2)

            def project_part(m, i, n0, n1):
                g, kind, part = i // 6, (i % 6) // 2, i % 2
                bank = bank_of(m, i)
                last = None
                if kind < 2:
                    for n in range(n0, n1):
                        (a, b), k = PARTS[n // KC], n % KC
                        last = nc.tensor.matmul(bank[:, :], ws[kind][a][:, k, g * P:(g + 1) * P],
                                                z[b][:, k, part * BANK:(part + 1) * BANK],
                                                start=n == 0, stop=n == 8)
                else:
                    tiles = range(*{(0, 5): (0, 2), (5, 9): (2, 4), (0, 9): (0, 4)}[n0, n1])
                    for t in tiles:
                        at = (part * 4 + t) * P
                        for n in range(9):
                            (a, b), k = PARTS[n // KC], n % KC
                            last = nc.tensor.matmul(bank[:, t * P:(t + 1) * P], z[a][:, k, at:at + P],
                                                    ws[2][b][:, k, g * P:(g + 1) * P],
                                                    start=n == 0, stop=n == 8)
                if n1 == 9:
                    last.then_inc(proj_ready, 1)

            def out_project(b, i):
                h, j = i // KC, i % KC
                take(pj, o_moved, 6 * b + i + 1)
                pe.wait_ge(ahi_ready, 6 * b + 4 + h + 1)
                pe.wait_ge(alo_ready, 6 * b + 4 + h + 1)
                for n in range(9):
                    (a, c), k = PARTS[n // KC], n % KC
                    last = nc.tensor.matmul(pj[:, :], ws[3][a][:, k, j * P:(j + 1) * P],
                                            ao[c][:, k, h * BANK:(h + 1) * BANK],
                                            start=n == 0, stop=n == 8)
                last.then_inc(o_ready, 1)

            def scores(b, u, s):
                g, w = u // UNITS, u % UNITS
                half, kp = w // 4, w % 4
                if w == 0:
                    pe.wait_ge(row_loaded[s], 16 * (GROUPS * b + g + 1))
                for e in range(2):
                    kt = 2 * kp + e
                    n = 2 * s + e
                    wait(pe, exp_ready, SCORES * (IU * b + u) + n + 1 - NST)
                    nc.tensor.matmul(st[(SCORES * u + n) % NST][:, :],
                                     kst[g][0:MAXROW + 1, s, kt * P:(kt + 1) * P],
                                     qst[g][0:MAXROW + 1, s, half * BANK:(half + 1) * BANK],
                                     start=True, stop=True).then_inc(st_ready, 1)

            def max_scores(group, m, g, item):
                h, t, half = item // (2 * TILES), item // 2 % TILES, item % 2
                wait(pe, mx_taken, ITEMS * group + item - 1)
                if item % (2 * TILES) == 1:
                    wait(pe, row_ready, HG * group + h)
                if item == 0:
                    pe.wait_ge(stacked[g], STACKED * (m + 1))
                nc.tensor.matmul(mx[item % 2][:, :], qst[g][0:MAXROW, h, t * P:(t + 1) * P],
                                 kst[g][0:MAXROW, h, half * BANK:(half + 1) * BANK],
                                 start=True, stop=True).then_inc(mx_ready, 1)

            def turn(number, parity):
                pe.wait_ge(combined, number + 1)
                nc.tensor.transpose(mx[1][0:TILES, 0:P], nm[parity][:, :], ident[:, :]).then_inc(turned, 1)

            def weigh(b, u, e):
                g, w = u // UNITS, u % UNITS
                unit_no = IU * b + u
                kt = 2 * (w % 4) + e
                if e == 0:
                    pe.wait_ge(exp_ready, SCORES * (unit_no + 1))
                    if w % 4 == 0:
                        wait(pe, pv_moved, 6 * b + u // 4)
                        if w == 0:
                            pe.wait_ge(stacked[g], STACKED * (b + 1))
                for h in range(HG):
                    last = nc.tensor.matmul(pv[h * HEAD:(h + 1) * HEAD, :],
                                            v[g][:, kt, h * HEAD:(h + 1) * HEAD],
                                            ex[u % 2 * HG + h][:, e * BANK:(e + 1) * BANK],
                                            start=kt == 0, stop=kt == TILES - 1,
                                            tile_position=(0, h * HEAD))
                last.then_inc(pv_ready, 1)

            def sum_up(b, u):
                w = u % UNITS
                pe.wait_ge(pair_added, STEPS // 2 * (IU * b + u + 1))
                if w % 4 == 1:
                    wait(pe, sum_inverted, 4 * (6 * b + u // 4))
                for h in range(HG):
                    last = nc.tensor.matmul(sm[h * HEAD:(h + 1) * HEAD, :], ones[:, :],
                                            pair[HG + h][:, :], start=w % 4 == 1,
                                            stop=w % 4 == 3, tile_position=(0, h * HEAD))
                last.then_inc(sum_ready, 1)

            def prologue():
                pe.wait_ge(const_set, 1)
                for h in range(HALVES):
                    mean(0, h)
                for h in range(HALVES):
                    var(0, h)
                for i in range(NQKV):
                    project(0, i)
                    project_part(0, i, 0, 9)
                    for item in prologue_items(i):
                        if item == 0:
                            pe.wait_ge(c_loaded, 32)
                        max_scores(0, 0, 0, item)
                        h = item // (2 * TILES)
                        if item % (2 * TILES) == 2 * TILES - 1 and h < HG - 1:
                            turn(h, h % 2)
                for h in range(HALVES):
                    mean(1, h)
                pe.wait_ge(row_of_ones, 3)

            def unit(b, u, out_proj=True, norm=True, qkv=True, maxima=True, load=False):
                g, w = u // UNITS, u % UNITS
                group = GROUPS * b + g + 1
                image = b + 1 if g == GROUPS - 1 else b
                lag = (b, u - 1) if u else (b - 1, IU - 1)
                lagging = not (isinstance(b, int) and b == 0 and u == 0)
                if u == FIRST and qkv:
                    free[id(pj)] = (std_ready, 2 * b + 4)

                def maximum(s, e):
                    if maxima:
                        max_scores(group, image, (g + 1) % GROUPS, 8 * w + 2 * s + e)

                scores(b, u, 0)
                if u >= FIRST and qkv:
                    project(b + 1, u - FIRST)
                    project_part(b + 1, u - FIRST, 0, 5)
                if u < FIRST and out_proj:
                    out_project(b - 1, u)
                maximum(0, 0)
                if u >= FIRST and qkv:
                    project_part(b + 1, u - FIRST, 5, 9)
                if w == 0 or w % 2 == 0 and maxima:
                    turn(turn_of(b, u), turn_of(0, u) % 2)
                scores(b, u, 1)
                maximum(0, 1)
                if lagging:
                    weigh(*lag, 0)
                maximum(1, 0)
                maximum(1, 1)
                scores(b, u, 2)
                if lagging:
                    weigh(*lag, 1)
                maximum(2, 0)
                if norm and u in (1, 2):
                    var(b + 1, u - 1)
                if load and u in (21, 23):
                    mean(b + 2, u // 2 - 10)
                scores(b, u, 3)
                maximum(2, 1)
                if lagging and u % 2 == 0:
                    sum_up(*lag)
                maximum(3, 0)
                maximum(3, 1)

            def epilogue(b):
                weigh(b, IU - 1, 0)
                weigh(b, IU - 1, 1)
                sum_up(b, IU - 1)
                for i in range(6):
                    out_project(b, i)

            schedule(nc.tensor, prologue, unit, epilogue)

        @block.vector
        def _(dve):
            def centre(m, h, k):
                at = slice(h * BANK, (h + 1) * BANK)
                dve.wait_ge(mean_ready, 2 * m + h + 1)
                nc.vector.tensor_tensor(xl[:, k, at], xl[:, k, at], bank_of(m, h)[:, :],
                                        ALU.subtract).then_inc(centred, 1)

            def invert_std(m, h, quarter):
                at = slice(quarter * QUARTER, (quarter + 1) * QUARTER)
                dve.wait_ge(std_ready, 2 * m + h + 1)
                nc.vector.reciprocal(std[h][:, at], std[h][:, at]).then_inc(inv_ready, 1)

            def normalise(m, h, k):
                at = slice(h * BANK, (h + 1) * BANK)
                dve.wait_ge(inv_ready, 8 * m + 4 * h + 4)
                dve.wait_ge(squared, 2 * m + h + 1)
                nc.vector.tensor_tensor(xl[:, k, at], xl[:, k, at], std[h][:, :], ALU.mult
                                        ).then_inc(z_ready, 1)

            def z_low(m, h, k):
                at = slice(h * BANK, (h + 1) * BANK)
                dve.wait_ge(zhi_ready, 2 * m + h + 1)
                ins = nc.vector.tensor_tensor(z[1][:, k, at], xl[:, k, at], z[0][:, k, at],
                                              ALU.subtract)
                if k == KC - 1:
                    ins.then_inc(zlo_ready, 1)

            def stage_low(m, i):
                g, kind, part = i // 6, (i % 6) // 2, i % 2
                if kind == 2:
                    return
                dve.wait_ge(hi_staged, 12 * m + 4 * g + 2 * kind + part + 1)
                hi, lo = staged[g % 2][kind]
                at = slice(part * BANK, (part + 1) * BANK)
                nc.vector.scalar_tensor_tensor(lo[:, at], bank_of(m, i)[:, :], 1.0 / WSCALE, hi[:, at],
                                               ALU.mult, ALU.subtract).then_inc(lo_staged, 1)

            def take_max(group, item):
                h, t, half = item // (2 * TILES), item // 2 % TILES, item % 2
                dve.wait_ge(mx_ready, ITEMS * group + item + 1)
                nc.vector.reduce_max(mxp[h % 2][:, t, half:half + 1], mx[item % 2][:, :], AX_X
                                     ).then_inc(mx_taken, 1)

            def combine(number, parity):
                dve.wait_ge(mx_taken, 2 * TILES * (number + 1))
                wait(dve, turned, number - 1)
                nc.vector.reduce_max(nm[parity][:, :], mxp[parity][:, :, :], AX_X
                                     ).then_inc(combined, 1)

            def invert_sum(b, x, quarter):
                at = slice(quarter * QUARTER, (quarter + 1) * QUARTER)
                dve.wait_ge(sum_ready, 2 * (6 * b + x + 1))
                if quarter == 0:
                    wait(dve, att_ready, 6 * b + x)
                nc.vector.reciprocal(inv[:, at], sm[:, at]).then_inc(sum_inverted, 1)

            def attended(b, x):
                dve.wait_ge(sum_inverted, 4 * (6 * b + x + 1))
                dve.wait_ge(pv_moved, 6 * b + x + 1)
                nc.vector.tensor_tensor(pvs[:, :], pvs[:, :], inv[:, :], ALU.mult
                                        ).then_inc(att_ready, 1)

            def prologue():
                nc.vector.memset(mean_w[:, :], 1.0 / C)
                nc.vector.memset(ones[:, :], 1.0).then_inc(const_set, 1)
                nc.vector.memset(eps[:, :], EPS).then_inc(const_set, 1)

                def weight_low(n):
                    dve.wait_ge(w_high, n + 1)
                    h, l = (t[:, :, :].rearrange("p k n -> p (k n)") for t in ws[n])
                    nc.vector.scalar_tensor_tensor(l, stage_w[n], WSCALE, h, ALU.mult,
                                                   ALU.subtract).then_inc(w_low, 1)

                for h in range(HALVES):
                    for k in range(KC):
                        centre(0, h, k)
                weight_low(0)
                for quarter in range(4):
                    invert_std(0, 0, quarter)
                for k in range(KC):
                    normalise(0, 0, k)
                weight_low(1)
                for k in range(KC):
                    z_low(0, 0, k)
                for quarter in range(4):
                    invert_std(0, 1, quarter)
                for k in range(KC):
                    normalise(0, 1, k)
                weight_low(2)
                for k in range(KC):
                    z_low(0, 1, k)
                weight_low(3)
                for i in range(NQKV):
                    if not prologue_items(i):
                        stage_low(0, i)
                    for item in prologue_items(i):
                        take_max(0, item)
                        if item == prologue_items(i)[0]:
                            stage_low(0, i)
                        h = item // (2 * TILES)
                        if item % (2 * TILES) == 2 * TILES - 1 and h < HG - 1:
                            combine(h, h % 2)
                for h in range(HALVES):
                    for k in range(KC):
                        centre(1, h, k)

            def unit(b, u, out_proj=True, norm=True, qkv=True, maxima=True, load=False):
                g, w = u // UNITS, u % UNITS
                group = GROUPS * b + g + 1
                started = not (isinstance(b, int) and b == 0 and u < 4)

                def maximum(s, e):
                    if maxima:
                        take_max(group, 8 * w + 2 * s + e)
                    elif u % 2 and e == 1:
                        dve.wait_ge(pair_ready, STEPS * (IU * b + u) + s + 1)
                        both = pair[HG + s]
                        nc.vector.tensor_tensor(both[:, :], both[:, :], pair[s][:, :], ALU.add
                                                ).then_inc(pair_added, 1)

                def beside(n):
                    if not maxima:
                        if u % 4 == 1 and n == 0:
                            for quarter in range(4):
                                invert_sum(b, (u - 5) // 4, quarter)
                            attended(b, (u - 5) // 4)
                        return
                    if started and u % 4 == 1 and n in (0, 1, 7):
                        invert_sum(b, (u - 5) // 4, min(n, 2))
                    if started and u % 4 == 2 and n == 0:
                        invert_sum(b, (u - 6) // 4, 3)
                        attended(b, (u - 6) // 4)
                    if n == 3 and u >= FIRST and qkv:
                        stage_low(b + 1, u - FIRST)
                    if load and u in (21, 23) and n in (5, 6):
                        for k in range(n - 5, 2 * n - 9):
                            centre(b + 2, u // 2 - 10, k)
                    if not norm:
                        return
                    if u == 2 and n in (1, 2, 4, 6):
                        invert_std(b + 1, 0, n // 2)
                    if u == 3 and n in (0, 1, 6):
                        invert_std(b + 1, 1, min(n, 2))
                    if u == 3 and n in (2, 3, 4):
                        normalise(b + 1, 0, n - 2)
                    if u == 4 and n == 0:
                        invert_std(b + 1, 1, 3)
                    if u == 4 and n in (2, 4, 6):
                        normalise(b + 1, 1, n // 2 - 1)
                    if (u, n) in ((4, 1), (5, 2), (5, 4)):
                        z_low(b + 1, 0, n // 2)
                    if u == 6 and n in (1, 3, 5):
                        z_low(b + 1, 1, n // 2)

                if w == 0 or w % 2 == 0 and maxima:
                    combine(turn_of(b, u), turn_of(0, u) % 2)
                for n in range(2 * STEPS):
                    beside(n)
                    maximum(n // 2, n % 2)

            def epilogue(b):
                for quarter in range(4):
                    invert_sum(b, 5, quarter)
                attended(b, 5)

            schedule(nc.vector, prologue, unit, epilogue)

        @block.scalar
        def _(act):
            def square(m, h):
                act.wait_ge(centred, KC * (2 * m + h + 1))
                wait(act, sq_folded, 4 * m + 2 * h)
                wait(act, proj_ready, NQKV * m)
                nc.scalar.activation(sq[:, :, :], xl[:, :, h * BANK:(h + 1) * BANK], ACT.Square
                                     ).then_inc(squared, 1)

            def root(m, h):
                act.wait_ge(var_ready, 2 * m + h + 1)
                nc.scalar.activation(std[h][:, :], bank_of(m, h)[:, :], ACT.Sqrt, bias=eps[:, 0:1]
                                     ).then_inc(std_ready, 1)

            def z_high(m, h):
                act.wait_ge(z_ready, 6 * m + 3 * h + 3)
                wait(act, proj_ready, NQKV * m)
                at = slice(h * BANK, (h + 1) * BANK)
                nc.scalar.activation(z[0][:, :, at], xl[:, :, at], ACT.Copy).then_inc(zhi_ready, 1)

            def stage_high(m, i):
                g, kind, part = i // 6, (i % 6) // 2, i % 2
                act.wait_ge(proj_ready, NQKV * m + i + 1)
                if i % 6 == 0:
                    if g == 2:
                        act.wait_ge(stacked[0], STACKED * (m + 1))
                    else:
                        wait(act, stacked[2 if g == 0 else 1], STACKED * m)
                if i % 6 == 4:
                    if g == 0:
                        wait(act, stacked[2], STACKED * m)
                    else:
                        act.wait_ge(stacked[g - 1], STACKED * (m + 1))
                if kind == 2:
                    nc.scalar.activation(vstaged[:, 4 * part:4 * part + 4, :],
                                         bank_of(m, i)[:, :].rearrange("p (t n) -> p t n", n=P), ACT.Copy,
                                         scale=1.0 / WSCALE).then_inc(v_staged, 1)
                else:
                    at = slice(part * BANK, (part + 1) * BANK)
                    nc.scalar.activation(staged[g % 2][kind][0][:, at], bank_of(m, i)[:, :], ACT.Copy,
                                         scale=1.0 / WSCALE).then_inc(hi_staged, 1)

            def row(number, h):
                act.wait_ge(turned, number + 1)
                if h >= 2:
                    act.wait_ge(row_loaded[h - 2], 4 * (number - h) + 16)
                else:
                    wait(act, row_loaded[h + 2], 4 * (number - h))
                nc.scalar.activation(mr[h % 2][:, :], mx[1][0:TILES, 0:P], ACT.Copy, scale=-1.0
                                     ).then_inc(row_ready, 1)

            def exponentials(b, u, s):
                unit_no = IU * b + u
                if not (isinstance(b, int) and b == 0 and u < 2):
                    act.wait_ge(pv_ready, 2 * unit_no - 2)
                    act.wait_ge(pair_ready, STEPS * unit_no + s - 2 * STEPS + 1)
                for e in range(2):
                    n = 2 * s + e
                    act.wait_ge(st_ready, SCORES * unit_no + n + 1)
                    nc.scalar.activation(ex[u % 2 * HG + s][:, e * BANK:(e + 1) * BANK],
                                         st[(SCORES * u + n) % NST][:, :], ACT.Exp,
                                         scale=SCALE).then_inc(exp_ready, 1)

            def move_pv(b, x):
                act.wait_ge(pv_ready, 8 * (6 * b + x + 1))
                wait(act, alo_ready, 6 * b + x)
                wait(act, ahi_ready, 6 * b + x)
                nc.scalar.activation(pvs[:, :], pv[:, :], ACT.Copy).then_inc(pv_moved, 1)

            def attended_high(b, x):
                g, h = x // 2 % GROUPS, x % 2
                act.wait_ge(att_ready, 6 * b + x + 1)
                nc.scalar.activation(ao[0][:, g, h * BANK:(h + 1) * BANK], pvs[:, :], ACT.Copy
                                     ).then_inc(ahi_ready, 1)

            def move_out(b, i):
                act.wait_ge(o_ready, 6 * b + i + 1)
                if i:
                    act.wait_ge(o_added, 6 * b + i)
                nc.scalar.activation(ot[:, :], pj[:, :], ACT.Identity, bias=bo[:, i % KC:i % KC + 1],
                                     scale=1.0 / WSCALE).then_inc(o_moved, 1)

            def prologue():
                act.wait_ge(const_set, 2)
                act.wait_ge(c_loaded, 32)

                def weight_high(n):
                    act.wait_ge(w_loaded[n], 16)
                    nc.scalar.activation(ws[n][0][:, :, :].rearrange("p k n -> p (k n)"), stage_w[n],
                                         ACT.Copy, scale=WSCALE).then_inc(w_high, 1)

                square(0, 0)
                weight_high(0)
                root(0, 0)
                square(0, 1)
                weight_high(1)
                root(0, 1)
                z_high(0, 0)
                weight_high(2)
                z_high(0, 1)
                weight_high(3)
                for i in range(NQKV):
                    stage_high(0, i)
                    for item in prologue_items(i):
                        h = item // (2 * TILES)
                        if item % (2 * TILES) == 2 * TILES - 1 and h < HG - 1:
                            row(h, h)

            def unit(b, u, out_proj=True, norm=True, qkv=True, maxima=True, load=False):
                w = u % UNITS
                started = not (isinstance(b, int) and b == 0 and u < 4)
                exponentials(b, u, 0)
                if w == 0:
                    row(turn_of(b, u), HG - 1)
                elif w % 2 == 0 and maxima:
                    row(turn_of(b, u), w // 2 - 1)
                if started and u % 4 == 2:
                    attended_high(b, (u - 6) // 4)
                exponentials(b, u, 1)
                if norm and u == 0:
                    square(b + 1, 0)
                if u >= FIRST and qkv:
                    stage_high(b + 1, u - FIRST)
                if u < FIRST and out_proj:
                    move_out(b - 1, u)
                if norm and u == 1:
                    square(b + 1, 1)
                exponentials(b, u, 2)
                if norm and u in (1, 2):
                    root(b + 1, u - 1)
                exponentials(b, u, 3)
                if started and u % 4 == 0:
                    move_pv(b, (u - 4) // 4)
                if norm and u in (3, 4):
                    z_high(b + 1, u - 3)

            def epilogue(b):
                move_pv(b, 5)
                attended_high(b, 5)
                for i in range(6):
                    move_out(b, i)

            schedule(nc.scalar, prologue, unit, epilogue)

        @block.gpsimd
        def _(pool):
            def attended_low(b, x):
                g, h = x // 2 % GROUPS, x % 2
                at = slice(h * BANK, (h + 1) * BANK)
                pool.wait_ge(att_ready, 6 * b + x + 1)
                pool.wait_ge(ahi_ready, 6 * b + x + 1)
                nc.gpsimd.tensor_tensor(ao[1][:, g, at], pvs[:, :], ao[0][:, g, at], ALU.subtract
                                        ).then_inc(alo_ready, 1)

            def add(b, i):
                h, j = i // KC, i % KC
                at = slice(h * BANK, (h + 1) * BANK)
                pool.wait_ge(o_moved, 6 * b + i + 1)
                if i == 0:
                    pool.wait_ge(r_loaded, 16 * (b + 1))
                nc.gpsimd.tensor_tensor(xr[:, j, at], xr[:, j, at], ot[:, :], ALU.add
                                        ).then_inc(o_added, 1)

            def fold(source, h, done, count):
                nc.gpsimd.tensor_tensor(xs[h][:, :], source[:, 0, :], source[:, 1, :], ALU.add
                                        ).then_inc(done, 1)
                pool.wait_ge(done, count + 1)
                nc.gpsimd.tensor_tensor(xs[h][:, :], xs[h][:, :], source[:, 2, :], ALU.add
                                        ).then_inc(done, 1)

            def fold_x(m, h):
                if h == 0:
                    pool.wait_ge(x_loaded, 16 * (m + 1))
                wait(pool, z_ready, 6 * (m - 1) + 3 * h + 3)
                fold(xl[:, :, h * BANK:(h + 1) * BANK], h, x_folded, 4 * m + 2 * h)

            def fold_squares(m, h):
                pool.wait_ge(squared, 2 * m + h + 1)
                pool.wait_ge(mean_ready, 2 * m + h + 1)
                fold(sq, h, sq_folded, 4 * m + 2 * h)

            def prologue():
                for h in range(HALVES):
                    fold_x(0, h)
                for h in range(HALVES):
                    fold_squares(0, h)
                pool.wait_ge(sq_folded, 4)
                for g in range(GROUPS):
                    nc.gpsimd.memset(kst[g][MAXROW:MAXROW + 1, :, :], 1.0).then_inc(row_of_ones, 1)
                    pool.wait_ge(row_of_ones, g + 1)
                for h in range(HALVES):
                    fold_x(1, h)

            def unit(b, u, out_proj=True, norm=True, maxima=True, load=False, **_flags):
                unit_no = IU * b + u
                started = not (isinstance(b, int) and b == 0 and u < 4)
                for s in range(STEPS):
                    if load and u in (18, 20) and s == 1:
                        fold_x(b + 2, u // 2 - 9)
                    if norm and u in (0, 1) and s == 3:
                        fold_squares(b + 1, u)
                    if started and u % 4 == 2 and s == 1:
                        attended_low(b, (u - 6) // 4)
                    if u < FIRST and out_proj and s == 2:
                        add(b - 1, u)
                    pool.wait_ge(exp_ready, SCORES * unit_no + 2 * s + 2)
                    if u % 2 and s == 0:
                        wait(pool, sum_ready, IU // 2 * b + u // 2)
                    if u % 2 == 0 and not (isinstance(b, int) and b == 0 and u == 0):
                        pool.wait_ge(pair_added, STEPS // 2 * (unit_no - 2) + s + 1)
                    e, both = ex[u % 2 * HG + s], pair[u % 2 * HG + s]
                    nc.gpsimd.tensor_tensor(both[:, :], e[:, 0:BANK], e[:, BANK:NPIX], ALU.add
                                            ).then_inc(pair_ready, 1)
                    if u % 2 and maxima:
                        pool.wait_ge(pair_ready, STEPS * unit_no + s + 1)
                        nc.gpsimd.tensor_tensor(both[:, :], both[:, :], pair[s][:, :], ALU.add
                                                ).then_inc(pair_added, 1)

            def epilogue(b):
                attended_low(b, 5)
                for i in range(6):
                    add(b, i)

            schedule(nc.gpsimd, prologue, unit, epilogue)


def ffn_stage(nc, x_in, w_in, b_in, w_out, out, n_images):
    HID = w_in.shape[1]
    MC = HID // P
    LAG = 2
    NH, NG, NS = 3, 3, 4
    EPS = 1e-5
    ctx = ExitStack()
    with ctx:
        N = Names(nc, ctx, "c")
        stage_i = N.sb("stage_i", [P, KC, HID])
        stage_o = N.sb("stage_o", [P, MC, C])
        wi = [N.sb(f"wi{s}", [P, KC, HID], F16) for s in range(2)]
        wo = [N.sb(f"wo{s}", [P, MC, C], F16) for s in range(2)]
        bias = N.sb("bias", [P, MC])
        mean_w = N.sb("mean_w", [P, P])
        eps = N.sb("eps", [P, 1])
        x = [N.sb(f"x{p}", [P, KC, BANK]) for p in range(2)]
        d = N.sb("d", [P, KC, BANK])
        sq = N.sb("sq", [P, KC, BANK])
        xs = N.sb("xs", [P, BANK])
        std = N.sb("std", [P, BANK])
        z = [[N.sb(f"z{p}{s}", [P, KC, BANK], F16) for s in range(2)] for p in range(2)]
        g = [N.sb(f"g{k}", [P, BANK]) for k in range(NG)]
        gs = [[N.sb(f"gs{k}{s}", [P, BANK], F16) for s in range(2)] for k in range(NS)]
        ob = [N.sb(f"ob{p}", [P, KC, BANK]) for p in range(2)]
        hid = [N.ps(f"hid{k}", [P, BANK]) for k in range(NH)]
        acc = [N.ps(f"acc{k}", [P, BANK]) for k in range(KC)]
        stat = [N.ps(f"stat{k}", [P, BANK]) for k in range(2)]

        i_loaded = N.sem("i_loaded")
        i_high = N.sem("i_high")
        i_low = N.sem("i_low")
        o_loaded = N.sem("o_loaded")
        o_high = N.sem("o_high")
        o_low = N.sem("o_low")
        b_loaded = N.sem("b_loaded")
        const_set = N.sem("const_set")
        x_loaded = [N.sem(f"x_loaded{p}") for p in range(2)]
        stored = [N.sem(f"stored{p}") for p in range(2)]
        folded = N.sem("folded")
        mean_ready = N.sem("mean_ready")
        centred = N.sem("centred")
        squared = N.sem("squared")
        var_ready = N.sem("var_ready")
        std_ready = N.sem("std_ready")
        inv_ready = N.sem("inv_ready")
        z_ready = N.sem("z_ready")
        zhi_ready = N.sem("zhi_ready")
        zlo_ready = N.sem("zlo_ready")
        hid_ready = N.sem("hid_ready")
        gelu_ready = N.sem("gelu_ready")
        ghi_ready = N.sem("ghi_ready")
        glo_ready = N.sem("glo_ready")
        out_used = N.sem("out_used")
        evicted = N.sem("evicted")
        block = ctx.enter_context(nc.Block())

        T = 2 * n_images

        def tiles(eng, body):
            body(0, 0, True, False)
            body(1, 1, False, False)
            body(2, 0, False, False)
            with eng.Fori(1, n_images - 1) as image:
                body(2 * image + 1, 1, False, False)
                body(2 * image + 2, 0, False, False)
            body(T - 1, 1, False, True)

        @block.sync
        def _(sp):
            sp.dma_start(x[0][:, :, :], image_tile(x_in, 0, 0, BANK)).then_inc(x_loaded[0], 16)
            sp.dma_start(stage_i[:, :, :], w_in.rearrange("(k p) n -> p k n", p=P)
                         ).then_inc(i_loaded, 16)
            sp.dma_start(stage_o[:, :, :], w_out.rearrange("(k p) n -> p k n", p=P)
                         ).then_inc(o_loaded, 16)
            sp.dma_start(bias[:, :], b_in).then_inc(b_loaded, 16)
            sp.dma_start(x[1][:, :, :], image_tile(x_in, 0, BANK, BANK)).then_inc(x_loaded[1], 16)

            def turn(image, p, load):
                sp.wait_ge(evicted, KC * (2 * image + p + 1))
                if load:
                    sp.dma_start(x[p][:, :, :], image_tile(x_in, image + 1, BANK * p, BANK)
                                 ).then_inc(x_loaded[p], 16)
                sp.dma_start(image_tile(out, image, BANK * p, BANK), ob[p][:, :, :]
                             ).then_inc(stored[p], 16)

            with sp.Fori(0, n_images - 1) as image:
                turn(image, 0, True)
                turn(image, 1, True)
            turn(n_images - 1, 0, False)
            turn(n_images - 1, 1, False)
            for p in range(2):
                sp.wait_ge(stored[p], 16 * n_images)

        @block.tensor
        def _(pe):
            def mean(t):
                pe.wait_ge(folded, 4 * t + 2)
                wait(pe, centred, t)
                nc.tensor.matmul(stat[0][:, :], mean_w[:, :], xs[:, :], start=True, stop=True
                                 ).then_inc(mean_ready, 1)

            def var(t):
                pe.wait_ge(folded, 4 * t + 4)
                wait(pe, std_ready, t)
                nc.tensor.matmul(stat[1][:, :], mean_w[:, :], xs[:, :], start=True, stop=True
                                 ).then_inc(var_ready, 1)

            def up(t, p, m):
                u = t * MC + m
                if m == 0:
                    pe.wait_ge(zlo_ready, t + 1)
                    if isinstance(t, int) and t == 0:
                        pe.wait_ge(i_low, KC)
                wait(pe, gelu_ready, u + 1 - NH)
                n = 0
                for a, b in PARTS:
                    for k in range(KC):
                        last = nc.tensor.matmul(hid[m % NH][:, :], wi[a][:, k, m * P:(m + 1) * P],
                                                z[p][b][:, k, :], start=n == 0, stop=n == 8)
                        n += 1
                last.then_inc(hid_ready, 1)

            def down(t, m):
                u = t * MC + m
                pe.wait_ge(ghi_ready, u + 1)
                pe.wait_ge(glo_ready, u + 1)
                if isinstance(t, int) and t == 0 and m == 0:
                    pe.wait_ge(o_low, 1)
                for j in range(KC):
                    if m == 0:
                        wait(pe, evicted, KC * t - KC + j + 1)
                    for n, (a, b) in enumerate(PARTS):
                        last = nc.tensor.matmul(acc[j][:, :], wo[a][:, m, j * P:(j + 1) * P],
                                                gs[m % NS][b][:, :], start=m == 0 and n == 0,
                                                stop=m == MC - 1 and n == 2)
                last.then_inc(out_used, 1)

            def body(t, p, first, last):
                for m in range(MC):
                    up(t, p, m)
                    if m >= LAG:
                        down(t, m - LAG)
                    elif not first:
                        down(t - 1, MC + m - LAG)
                    if not last and m == 4:
                        mean(t + 1)
                    if not last and m == 7:
                        var(t + 1)
                if last:
                    for m in range(MC - LAG, MC):
                        down(t, m)

            pe.wait_ge(const_set, 1)
            mean(0)
            var(0)
            tiles(nc.tensor, body)

        @block.vector
        def _(dve):
            nc.vector.memset(mean_w[:, :], 1.0 / C)
            nc.vector.memset(eps[:, :], EPS).then_inc(const_set, 1)

            def centre(t, p):
                dve.wait_ge(mean_ready, t + 1)
                wait(dve, zlo_ready, t)
                wait(dve, zhi_ready, t)
                nc.vector.tensor_tensor(d[:, :, :], x[p][:, :, :],
                                        stat[0][:, None, :].broadcast_to([P, KC, BANK]),
                                        ALU.subtract).then_inc(centred, 1)

            def invert(t):
                dve.wait_ge(std_ready, t + 1)
                nc.vector.reciprocal(std[:, :], std[:, :]).then_inc(inv_ready, 1)

            def normalise(t):
                dve.wait_ge(inv_ready, t + 1)
                dve.wait_ge(squared, t + 1)
                nc.vector.tensor_tensor(d[:, :, :], d[:, :, :],
                                        std[:, None, :].broadcast_to([P, KC, BANK]),
                                        ALU.mult).then_inc(z_ready, 1)

            def low(t, p):
                dve.wait_ge(z_ready, t + 1)
                dve.wait_ge(zhi_ready, t + 1)
                nc.vector.tensor_tensor(z[p][1][:, :, :], d[:, :, :], z[p][0][:, :, :],
                                        ALU.subtract).then_inc(zlo_ready, 1)

            def gelu_low(t, m):
                u = t * MC + m
                dve.wait_ge(ghi_ready, u + 1)
                wait(dve, out_used, u + 1 - NS)
                nc.vector.tensor_tensor(gs[m % NS][1][:, :], g[m % NG][:, :], gs[m % NS][0][:, :],
                                        ALU.subtract).then_inc(glo_ready, 1)

            def evict(t, p):
                dve.wait_ge(out_used, (t + 1) * MC)
                if isinstance(t, int):
                    wait(dve, stored[p], 16 * ((t - p) // 2))
                else:
                    dve.wait_ge(stored[p], 8 * (t - p))
                for j in range(KC):
                    nc.vector.scalar_tensor_tensor(ob[p][:, j, :], acc[j][:, :], 1.0 / WSCALE,
                                                   x[p][:, j, :], ALU.mult, ALU.add
                                                   ).then_inc(evicted, 1)

            def body(t, p, first, last):
                for m in range(MC):
                    gelu_low(t, m)
                    if m == 1 and not first:
                        evict(t - 1, 1 - p)
                    if not last:
                        if m == 5:
                            centre(t + 1, 1 - p)
                        if m == 8:
                            invert(t + 1)
                            normalise(t + 1)
                        if m == 10:
                            low(t + 1, 1 - p)
                if last:
                    evict(t, p)

            centre(0, 0)
            for k in range(KC):
                dve.wait_ge(i_high, k + 1)
                nc.vector.scalar_tensor_tensor(wi[1][:, k, :], stage_i[:, k, :], WSCALE,
                                               wi[0][:, k, :], ALU.mult, ALU.subtract
                                               ).then_inc(i_low, 1)
                if k == 1:
                    invert(0)
                    normalise(0)
            low(0, 0)
            dve.wait_ge(o_high, 1)
            nc.vector.scalar_tensor_tensor(wo[1][:, :, :], stage_o[:, :, :], WSCALE, wo[0][:, :, :],
                                           ALU.mult, ALU.subtract).then_inc(o_low, 1)
            tiles(nc.vector, body)

        @block.scalar
        def _(act):
            def square(t):
                act.wait_ge(centred, t + 1)
                wait(act, folded, 4 * t)
                nc.scalar.activation(sq[:, :, :], d[:, :, :], ACT.Square).then_inc(squared, 1)

            def root(t):
                act.wait_ge(var_ready, t + 1)
                wait(act, z_ready, t)
                nc.scalar.activation(std[:, :], stat[1][:, :], ACT.Sqrt, bias=eps[:, 0:1]
                                     ).then_inc(std_ready, 1)

            def high(t, p):
                act.wait_ge(z_ready, t + 1)
                wait(act, hid_ready, (t - 1) * MC)
                nc.scalar.activation(z[p][0][:, :, :], d[:, :, :], ACT.Copy).then_inc(zhi_ready, 1)

            def gelu(t, m):
                u = t * MC + m
                act.wait_ge(hid_ready, u + 1)
                wait(act, glo_ready, u + 1 - NG)
                wait(act, out_used, u + 1 - NS)
                nc.scalar.activation(g[m % NG][:, :], hid[m % NH][:, :], ACT.Gelu,
                                     bias=bias[:, m:m + 1], scale=1.0 / WSCALE
                                     ).then_inc(gelu_ready, 1)
                act.wait_ge(gelu_ready, u + 1)
                nc.scalar.activation(gs[m % NS][0][:, :], g[m % NG][:, :], ACT.Copy
                                     ).then_inc(ghi_ready, 1)

            def body(t, p, first, last):
                for m in range(MC):
                    gelu(t, m)
                    if not last:
                        if m == 5:
                            square(t + 1)
                        if m == 8:
                            root(t + 1)
                        if m == 9:
                            high(t + 1, 1 - p)

            act.wait_ge(const_set, 1)
            square(0)
            act.wait_ge(i_loaded, 16)
            for k in range(KC):
                nc.scalar.activation(wi[0][:, k, :], stage_i[:, k, :], ACT.Copy, scale=WSCALE
                                     ).then_inc(i_high, 1)
                if k == 0:
                    root(0)
            high(0, 0)
            act.wait_ge(o_loaded, 16)
            nc.scalar.activation(wo[0][:, :, :], stage_o[:, :, :], ACT.Copy, scale=WSCALE
                                 ).then_inc(o_high, 1)
            act.wait_ge(b_loaded, 16)
            tiles(nc.scalar, body)

        @block.gpsimd
        def _(pool):
            def fold(t, source, n):
                nc.gpsimd.tensor_tensor(xs[:, :], source[:, 0, :], source[:, 1, :], ALU.add
                                        ).then_inc(folded, 1)
                pool.wait_ge(folded, 4 * t + n + 1)
                nc.gpsimd.tensor_tensor(xs[:, :], xs[:, :], source[:, 2, :], ALU.add
                                        ).then_inc(folded, 1)

            def body(t, p, first, last):
                if last:
                    return
                t, p = t + 1, 1 - p
                pool.wait_ge(x_loaded[p], 16 * ((t - p) // 2 + 1) if isinstance(t, int)
                             else 8 * (t - p) + 16)
                wait(pool, var_ready, t)
                fold(t, x[p], 0)
                pool.wait_ge(squared, t + 1)
                pool.wait_ge(mean_ready, t + 1)
                fold(t, sq, 2)

            body(-1, 1, False, False)
            tiles(nc.gpsimd, body)


def program(nc, x, conv_main, conv_corr, group_mean, masks, selectors, corr_start,
            w_q, w_k, w_v, w_o, b_o, identity, w_in, b_in, w_out, out):
    n_images = x.shape[0]
    after_conv = nc.dram_tensor("after_conv", [n_images, C, NPIX], F32, kind="Internal").ap()
    after_attention = nc.dram_tensor("after_attention", [n_images, C, NPIX], F32,
                                     kind="Internal").ap()
    conv_stage(nc, x, conv_main, conv_corr, group_mean, masks, selectors, corr_start,
               after_conv, n_images)
    attention_stage(nc, after_conv, w_q, w_k, w_v, w_o, b_o, identity, after_attention, n_images)
    ffn_stage(nc, after_attention, w_in, b_in, w_out, out, n_images)


def kernel(x, L0_conv_conv_w, L0_conv_conv_b, L1_attn_Wq, L1_attn_Wk, L1_attn_Wv, L1_attn_Wo,
           L1_attn_bo, L1_ffn_in_weight, L1_ffn_in_bias, L1_ffn_out_weight):
    import numpy as np
    import concourse.bacc as bacc
    from concourse.bass_utils import run_bass_kernel_spmd

    def per_partition(bias):
        return np.asarray(bias).reshape(-1, P).T

    x = np.asarray(x)
    conv_w = np.asarray(L0_conv_conv_w)
    corr = [conv_w[:, C + at] for at in corr_weight_rows()] + [np.asarray(L0_conv_conv_b)]
    constants = conv_constants()
    arrays = {
        "x": x.reshape(x.shape[0], C, NPIX),
        "conv_main": conv_w[:, :C].T,
        "conv_corr": np.stack(corr),
        **constants,
        "w_q": np.asarray(L1_attn_Wq).T,
        "w_k": np.asarray(L1_attn_Wk).T,
        "w_v": np.asarray(L1_attn_Wv).T,
        "w_o": np.asarray(L1_attn_Wo).T,
        "b_o": per_partition(L1_attn_bo),
        "identity": np.eye(P, dtype=np.float32),
        "w_in": np.asarray(L1_ffn_in_weight).T,
        "b_in": per_partition(L1_ffn_in_bias),
        "w_out": np.asarray(L1_ffn_out_weight),
    }
    arrays = {f"in_{name}": np.ascontiguousarray(a) for name, a in arrays.items()}
    nc = bacc.Bacc("TRN2", target_bir_lowering=False, num_devices=1)
    args = [nc.dram_tensor(name, a.shape, mybir.dt.from_np(a.dtype), kind="ExternalInput").ap()
            for name, a in arrays.items()]
    out = nc.dram_tensor("out", [x.shape[0], C, NPIX], F32, kind="ExternalOutput").ap()
    program(nc, *args, out)
    result = run_bass_kernel_spmd(nc, [arrays], core_ids=[0])
    return result.results[0]["out"].reshape(x.shape)
```
